# Optimizing a Trainium2 kernel written in Bass

```python
import numpy as np
import jax
import jax.numpy as jnp

def _softmax(x, axis=-1):
    return jax.nn.softmax(x, axis=axis)

def _gelu(x):
    return jax.nn.gelu(x, approximate=True)

def _silu(x):
    return jax.nn.silu(x)

def _sigmoid(x):
    return jax.nn.sigmoid(x)

def _layernorm(x, axis=-1, eps=1e-05):
    m = jnp.mean(x, axis=axis, keepdims=True)
    v = jnp.var(x, axis=axis, keepdims=True)
    return (x - m) / jnp.sqrt(v + eps)

def _scatter_add(tgt, idx, src, axis=0):
    return tgt.at[idx].add(src)

def _segment_sum(src, seg, n):
    return jax.ops.segment_sum(src, seg, n)
kernel_name = 'mk_macaron_d1_jaxref_r8_edc369'

def setup_inputs(seed: int=0):
    np.random.seed(seed)
    _w = jnp.asarray

    def _L0_attn_setup():
        import jax, jax.numpy as jnp
        import numpy as np
        D_MODEL = 128
        NUM_HEADS = 16
        B, S = (1, 512)
        key = jax.random.key(seed)
        kx, kq, kk, kv, ko = jax.random.split(key, 5)
        std = (1.0 / D_MODEL) ** 0.5

        def trunc(k):
            return std * jax.random.truncated_normal(k, -3.0, 3.0, (D_MODEL, D_MODEL), dtype=jnp.float32)
        return {'x': jax.random.normal(kx, (B, S, D_MODEL), dtype=jnp.float32), 'W_Q': trunc(kq), 'W_K': trunc(kk), 'W_V': trunc(kv), 'W_O': trunc(ko)}
    _L0_attn_in = _L0_attn_setup()

    def _L0_ffn_setup():
        import jax, jax.numpy as jnp
        import numpy as np
        NUM_EXPERTS = 8
        TOP_K = 2

        def _swiglu(x, w1, w2, w3):
            return jax.nn.silu(x @ w1) * (x @ w3) @ w2
        key = jax.random.key(seed)
        ks = jax.random.split(key, 9)
        B, S, D, H, E = (1, 128, 128, 128, NUM_EXPERTS)
        std = 0.02
        return {'x': jax.random.normal(ks[0], (B, S, D), jnp.float32), 'router_w': jax.random.normal(ks[1], (D, E), jnp.float32) * std, 'expert_bias': jnp.zeros((E,), jnp.float32), 'w1': jax.random.normal(ks[2], (E, D, H), jnp.float32) * std, 'w2': jax.random.normal(ks[3], (E, H, D), jnp.float32) * std, 'w3': jax.random.normal(ks[4], (E, D, H), jnp.float32) * std, 'sw1': jax.random.normal(ks[5], (D, H), jnp.float32) * std, 'sw2': jax.random.normal(ks[6], (H, D), jnp.float32) * std, 'sw3': jax.random.normal(ks[7], (D, H), jnp.float32) * std}
    _L0_ffn_in = _L0_ffn_setup()
    _d = {'L0_attn_x': _L0_attn_in['x'], 'L0_attn_W_Q': _L0_attn_in['W_Q'], 'L0_attn_W_K': _L0_attn_in['W_K'], 'L0_attn_W_V': _L0_attn_in['W_V'], 'L0_attn_W_O': _L0_attn_in['W_O'], 'L0_ffn_router_w': _L0_ffn_in['router_w'], 'L0_ffn_expert_bias': _L0_ffn_in['expert_bias'], 'L0_ffn_w1': _L0_ffn_in['w1'], 'L0_ffn_w2': _L0_ffn_in['w2'], 'L0_ffn_w3': _L0_ffn_in['w3'], 'L0_ffn_sw1': _L0_ffn_in['sw1'], 'L0_ffn_sw2': _L0_ffn_in['sw2'], 'L0_ffn_sw3': _L0_ffn_in['sw3']}
    _x0 = _d['L0_attn_x']
    _d['L0_attn_x'] = jax.random.normal(jax.random.fold_in(jax.random.key(seed), 1), (32, 256, 128), dtype=_x0.dtype)
    del _x0
    return _d

def reference(L0_attn_x, L0_attn_W_Q, L0_attn_W_K, L0_attn_W_V, L0_attn_W_O, L0_ffn_router_w, L0_ffn_expert_bias, L0_ffn_w1, L0_ffn_w2, L0_ffn_w3, L0_ffn_sw1, L0_ffn_sw2, L0_ffn_sw3):

    def _L0_attn_ref(x, W_Q, W_K, W_V, W_O):
        import jax, jax.numpy as jnp
        import numpy as np
        D_MODEL = 128
        NUM_HEADS = 16
        B, S = (1, 512)
        Bx, Sx, Dm = x.shape
        H = NUM_HEADS
        d_attn = Dm // H
        Q = x @ W_Q.T
        K = x @ W_K.T
        V = x @ W_V.T
        Q = Q.reshape(Bx, Sx, H, d_attn).transpose(0, 2, 1, 3)
        K = K.reshape(Bx, Sx, H, d_attn).transpose(0, 2, 1, 3)
        V = V.reshape(Bx, Sx, H, d_attn).transpose(0, 2, 1, 3)
        scale = 1.0 / jnp.sqrt(jnp.asarray(d_attn, dtype=x.dtype))
        attn = jnp.einsum('bhqd,bhkd->bhqk', Q, K) * scale
        causal = jnp.tril(jnp.ones((Sx, Sx), dtype=bool))
        attn = jnp.where(causal, attn, jnp.asarray(-jnp.inf, dtype=attn.dtype))
        probs = jax.nn.softmax(attn, axis=-1)
        y = jnp.einsum('bhqk,bhkd->bhqd', probs, V)
        y = y.transpose(0, 2, 1, 3).reshape(Bx, Sx, Dm)
        return y @ W_O.T

    def _L0_ffn_ref(x, router_w, expert_bias, w1, w2, w3, sw1, sw2, sw3):
        import jax, jax.numpy as jnp
        import numpy as np
        NUM_EXPERTS = 8
        TOP_K = 2

        def _swiglu(x, w1, w2, w3):
            return jax.nn.silu(x @ w1) * (x @ w3) @ w2
        B, S, D = x.shape
        E, K = (NUM_EXPERTS, TOP_K)
        N = B * S
        x_flat = x.reshape(N, D)
        logits = x_flat @ router_w
        scores = jax.nn.softmax(logits.astype(jnp.float32), axis=-1)
        _, sel = jax.lax.top_k(scores + expert_bias[None, :], K)
        top_scores = jnp.take_along_axis(scores, sel, axis=-1)
        flat_exp = sel.reshape(-1)
        order = jnp.argsort(flat_exp)
        exp_sorted = flat_exp[order]
        routed_input = x_flat[order // K]
        routed_output = jnp.zeros_like(routed_input)
        for e in range(E):
            mask = (exp_sorted == e)[:, None]
            y_e = _swiglu(routed_input, w1[e], w2[e], w3[e])
            routed_output = routed_output + jnp.where(mask, y_e, 0.0)
        unsorted = jnp.zeros((N * K, D), routed_output.dtype).at[order].set(routed_output)
        unsorted = unsorted.reshape(N, K, D)
        out_experts = jnp.einsum('nk,nkd->nd', top_scores, unsorted)
        shared_out = _swiglu(x_flat, sw1, sw2, sw3)
        return (shared_out + out_experts).reshape(B, S, D)
    x = L0_attn_x
    x = x + 0.5 * _L0_ffn_ref(_layernorm(x, axis=-1), L0_ffn_router_w, L0_ffn_expert_bias, L0_ffn_w1, L0_ffn_w2, L0_ffn_w3, L0_ffn_sw1, L0_ffn_sw2, L0_ffn_sw3)
    x = x + _L0_attn_ref(_layernorm(x, axis=-1), L0_attn_W_Q, L0_attn_W_K, L0_attn_W_V, L0_attn_W_O)
    x = x + 0.5 * _L0_ffn_ref(_layernorm(x, axis=-1), L0_ffn_router_w, L0_ffn_expert_bias, L0_ffn_w1, L0_ffn_w2, L0_ffn_w3, L0_ffn_sw1, L0_ffn_sw2, L0_ffn_sw3)
    return x

_drawn_inputs = setup_inputs


def setup_inputs(seed=0):
    import zlib

    import numpy as np

    out = dict(_drawn_inputs(seed))
    spreads = {'L0_ffn_expert_bias': (0.0, 0.8)}
    factors = {'L0_ffn_router_w': 8.0,
     'L0_ffn_w1': 8.0,
     'L0_ffn_w2': 8.0,
     'L0_ffn_w3': 8.0,
     'L0_ffn_sw1': 8.0,
     'L0_ffn_sw2': 8.0,
     'L0_ffn_sw3': 8.0}
    for name, (base, spread) in spreads.items():
        noise = np.random.default_rng([zlib.crc32(name.encode()), seed]).standard_normal(out[name].shape)
        drawn = base * np.exp(spread * noise) if base else spread * noise
        out[name] = jnp.asarray(drawn.astype(out[name].dtype))
    for name, factor in factors.items():
        out[name] = (out[name] * factor).astype(out[name].dtype)
    return out
```

```python
from contextlib import ExitStack

import concourse.bass as bass
from concourse import mybir

ALU = mybir.AluOpType
ACT = mybir.ActivationFunctionType
AX = mybir.AxisListType
F32 = mybir.dt.float32
F16 = mybir.dt.float16
BF16 = mybir.dt.bfloat16

P = 128
SEQ = 256
TILES = 4
CHUNK = TILES * P
CHUNKS = 32 * SEQ // CHUNK
EXPERTS = 8
STEPS = EXPERTS + 1
LAG = 3
LN_EPS = 1e-5
HEADS = 16
HEAD = P // HEADS
GROUPS = 4
ROWS = P // GROUPS
MAX_ROW = 3 * HEAD
SCALE = float(HEAD) ** -0.5
UNITS = 4
FAR = 1e30
GATE_PARTS = (0, 2, 7, 12, 17, 20)
GATE_STEPS = GATE_PARTS[-1]
DMA = 16


def run_pairs(eng, chunk):
    chunk(0, 0)
    chunk(1, 1)
    with eng.Fori(1, CHUNKS // 2 - 1) as pair:
        chunk(pair * 2, 0)
        chunk(pair * 2 + 1, 1)
    chunk(CHUNKS - 2, 0)
    chunk(CHUNKS - 1, 1)


def is_first(c):
    return isinstance(c, int) and c == 0


def is_last(c):
    return isinstance(c, int) and c == CHUNKS - 1


def exists(c):
    return not isinstance(c, int) or 0 <= c < CHUNKS


def wait_count(eng, sem, value):
    if not isinstance(value, int) or value > 0:
        eng.wait_ge(sem, value)


LN_STEPS = 2 * TILES


def norm_stats(dve, nc, c, x, buf, step, scaled):
    base = c * LN_STEPS
    wait_count(dve, scaled, c)
    for t in range(TILES):
        nc.vector.bn_stats(buf["stats"][:, t, :], x[:, c * TILES + t, :]).then_inc(step, 1)
    dve.wait_ge(step, base + TILES)
    nc.vector.memset(buf["spare"][:, :], 0.0)
    for t in range(TILES):
        nc.vector.bn_aggr(buf["moments"][:, t, :], buf["stats"][:, t, :]).then_inc(step, 1)


def norm_root(pool, nc, c, buf, step, rooted):
    pool.wait_ge(step, (c + 1) * LN_STEPS)
    nc.gpsimd.tensor_tensor(buf["var_eps"][:, :], buf["moments"][:, :, 1], buf["eps"][:, :], ALU.add).then_inc(rooted, 1)
    pool.wait_ge(rooted, 2 * c + 1)
    nc.gpsimd.tensor_tensor(buf["rstd"][:, :], buf["var_eps"][:, :], buf["power"][:, :], ALU.pow).then_inc(rooted, 1)


def norm_scale(dve, nc, c, x, buf, rooted, scaled):
    dve.wait_ge(rooted, 2 * c + 2)
    for t in range(TILES):
        last = nc.vector.tensor_scalar(buf["xn"][:, t, :], x[:, c * TILES + t, :], buf["moments"][:, t, 0:1],
                                       buf["rstd"][:, t:t + 1], ALU.subtract, ALU.mult)
    last.then_inc(scaled, 1)


def ffn_phase(nc, x, consts, w, phase, x_dram, out):
    with ExitStack() as ctx:
        def sb(name, shape, dt):
            return ctx.enter_context(nc.sbuf_tensor(f"{name}_{phase}", shape, dt))

        def bank(name):
            return ctx.enter_context(nc.psum_tensor(f"{name}_{phase}", [P, CHUNK], F32))

        def sem(name):
            return ctx.enter_context(nc.semaphore(f"{name}_{phase}"))

        ident, select_gate = consts["ident"], consts["select_gate"]
        buf = {
            "stats": sb("stats", [P, TILES, 6], F32), "moments": sb("moments", [P, TILES, 2], F32),
            "rstd": sb("rstd", [P, TILES], F32), "var_eps": sb("var_eps", [P, TILES], F32), "power": consts["power"],
            "eps": consts["eps"], "spare": sb("spare", [P, 1], F32),
            "xn": sb("xn", [P, TILES, P], F32),
        }
        xn = buf["xn"]
        xt_hi = [sb(f"xt_hi{s}", [P, CHUNK], F16) for s in range(2)]
        xt_lo = [sb(f"xt_lo{s}", [P, CHUNK], F16) for s in range(2)]
        silu = [sb(f"silu{s}", [P, CHUNK], F32) for s in range(2)]
        prod = sb("prod", [P, CHUNK], F32)
        h = [sb(f"h{s}", [P, CHUNK], F32) for s in range(3)]
        h_hi = [sb(f"h_hi{s}", [P, CHUNK], F16) for s in range(3)]
        h_lo = [sb(f"h_lo{s}", [P, CHUNK], F16) for s in range(3)]
        yt = sb("yt", [P, CHUNK], F32)
        gate_t = [sb(f"gate_t{s}", [2 * EXPERTS, CHUNK], F16) for s in range(2)]
        g = {n: sb(n, [P, TILES, EXPERTS], F32) for n in
             ("shifted", "expd", "score", "biased", "hit", "rank", "first", "rest", "second", "gate")}
        top = {n: sb(n, [P, TILES], F32) for n in ("peak", "total", "inverse", "best1", "who1", "best2", "who2")}
        gate_parts = sb("gate_parts", [P, TILES, 2 * EXPERTS], F16)

        a_bank = [bank(f"a{s}") for s in range(2)]
        b_bank = [bank(f"b{s}") for s in range(2)]
        gate_bank, y_bank, t_bank, r_bank = bank("gate_b"), bank("y_b"), bank("t_b"), bank("r_b")
        logits = r_bank[:, 0:TILES * EXPERTS].rearrange("p (t e) -> p t e", e=EXPERTS)
        gate_tp = r_bank[0:2 * EXPERTS, 256:512].bitcast(F16)

        ln_rooted = sem("ln_rooted")
        x_loaded = [sem(f"x_loaded{s}") for s in range(2)]
        ln_step, ln_done, xt_done, xhi_done, xlo_done = (
            sem(n) for n in ("ln_step", "ln_done", "xt_done", "xhi_done", "xlo_done"))
        logits_done, gate_step, expd_done, gates_done, gate_tp_done, gate_t_done = (
            sem(n) for n in ("logits_done", "gate_step", "expd_done", "gates_done", "gate_tp_done", "gate_t_done"))
        a_done, b_done, silu_done, prod_done, gate_b_done, h_done = (
            sem(n) for n in ("a_done", "b_done", "silu_done", "prod_done", "gate_b_done", "h_done"))
        hhi_done, hlo_done, w2_done, yt_done, y_tok_done, x_added, stored = (
            sem(n) for n in ("hhi_done", "hlo_done", "w2_done", "yt_done", "y_tok_done", "x_added", "stored"))

        block = ctx.enter_context(nc.Block())

        @block.sync
        def _(sp):
            if x_dram is not None:
                src = x_dram.rearrange("(c p) d -> p c d", p=P)
                for c in range(CHUNKS):
                    wait_count(sp, x_loaded[c % 2], c // 2 * DMA)
                    sp.dma_start(x[:, c * TILES:(c + 1) * TILES, :],
                                 src[:, c * TILES:(c + 1) * TILES, :]).then_inc(x_loaded[c % 2], DMA)
            if out is not None:
                dst = out.rearrange("(c p) d -> p c d", p=P)
                with sp.Fori(0, CHUNKS) as c:
                    sp.wait_ge(x_added, c + 1)
                    sp.dma_start(dst[:, bass.ds(c * TILES, TILES), :],
                                 x[:, bass.ds(c * TILES, TILES), :]).then_inc(stored, DMA)
                sp.wait_ge(stored, CHUNKS * DMA)

        @block.vector
        def _(dve):
            def norm(c, slot):
                if x_dram is not None:
                    dve.wait_ge(x_loaded[slot], ((c - slot) // 2 + 1) * DMA if isinstance(c, int)
                                else (c - slot) * (DMA // 2) + DMA)
                norm_stats(dve, nc, c, x, buf, ln_step, ln_done)

            def scale(c):
                wait_count(dve, xt_done, c)
                norm_scale(dve, nc, c, x, buf, ln_rooted, ln_done)

            def split_x(c, slot):
                dve.wait_ge(xhi_done, c + 1)
                nc.vector.tensor_tensor(xt_lo[slot][:, :], t_bank[:, :], xt_hi[slot][:, :],
                                        ALU.subtract).then_inc(xlo_done, 1)

            def gates(c, part):
                first, last = GATE_PARTS[part], GATE_PARTS[part + 1]
                if part > 0:
                    dve.wait_ge(gate_step, c * GATE_STEPS + first)
                done = [first]

                def then(ins):
                    done[0] += 1
                    ins.then_inc(gate_step, 1)
                    if done[0] < last:
                        dve.wait_ge(gate_step, c * GATE_STEPS + done[0])

                def wide(v):
                    return v[:, :].unsqueeze(2).to_broadcast([P, TILES, EXPERTS])

                bias = consts["bias"][:, :].unsqueeze(1).to_broadcast([P, TILES, EXPERTS])
                order = consts["order"][:, :].unsqueeze(1).to_broadcast([P, TILES, EXPERTS])
                if part == 0:
                    dve.wait_ge(logits_done, c + 1)
                    then(nc.vector.tensor_reduce(top["peak"][:, :], logits, AX.X, ALU.max))
                    then(nc.vector.tensor_tensor(g["shifted"][:, :, :], logits, wide(top["peak"]), ALU.subtract))
                if part == 1:
                    dve.wait_ge(expd_done, c + 1)
                    then(nc.vector.tensor_reduce(top["total"][:, :], g["expd"][:, :, :], AX.X, ALU.add))
                    then(nc.vector.reciprocal(top["inverse"][:, :], top["total"][:, :]))
                    then(nc.vector.tensor_tensor(g["score"][:, :, :], g["expd"][:, :, :], wide(top["inverse"]),
                                                 ALU.mult))
                    then(nc.vector.tensor_tensor(g["biased"][:, :, :], g["score"][:, :, :], bias, ALU.add))
                    then(nc.vector.tensor_reduce(top["best1"][:, :], g["biased"][:, :, :], AX.X, ALU.max))
                if part == 2:
                    then(nc.vector.tensor_tensor(g["hit"][:, :, :], g["biased"][:, :, :], wide(top["best1"]),
                                                 ALU.is_equal))
                    then(nc.vector.tensor_tensor(g["rank"][:, :, :], g["hit"][:, :, :], order, ALU.mult))
                    then(nc.vector.tensor_reduce(top["who1"][:, :], g["rank"][:, :, :], AX.X, ALU.max))
                    then(nc.vector.tensor_tensor(g["first"][:, :, :], g["rank"][:, :, :], wide(top["who1"]),
                                                 ALU.is_equal))
                    then(nc.vector.scalar_tensor_tensor(g["rest"][:, :, :], g["first"][:, :, :], -FAR,
                                                        g["biased"][:, :, :], ALU.mult, ALU.add))
                if part == 3:
                    then(nc.vector.tensor_reduce(top["best2"][:, :], g["rest"][:, :, :], AX.X, ALU.max))
                    then(nc.vector.tensor_tensor(g["hit"][:, :, :], g["rest"][:, :, :], wide(top["best2"]),
                                                 ALU.is_equal))
                    then(nc.vector.tensor_tensor(g["rank"][:, :, :], g["hit"][:, :, :], order, ALU.mult))
                    then(nc.vector.tensor_reduce(top["who2"][:, :], g["rank"][:, :, :], AX.X, ALU.max))
                    then(nc.vector.tensor_tensor(g["second"][:, :, :], g["rank"][:, :, :], wide(top["who2"]),
                                                 ALU.is_equal))
                if part == 4:
                    then(nc.vector.tensor_tensor(g["hit"][:, :, :], g["first"][:, :, :], g["second"][:, :, :],
                                                 ALU.add))
                    then(nc.vector.tensor_tensor(g["gate"][:, :, :], g["hit"][:, :, :], g["score"][:, :, :],
                                                 ALU.mult))
                    wait_count(dve, gate_tp_done, c)
                    then(nc.vector.tensor_copy(gate_parts[:, :, 0:EXPERTS], g["gate"][:, :, :]))
                    dve.wait_ge(gate_step, c * GATE_STEPS + done[0])
                    nc.vector.tensor_tensor(gate_parts[:, :, EXPERTS:2 * EXPERTS], g["gate"][:, :, :],
                                            gate_parts[:, :, 0:EXPERTS], ALU.subtract).then_inc(gates_done, 1)
                assert done[0] == last

            def swiglu(c, slot, e):
                n, k = c * STEPS + e, (slot + e) % 2
                dve.wait_ge(silu_done, n + 1)
                dve.wait_ge(b_done, n + 1)
                wait_count(dve, hhi_done, n - 2)
                wait_count(dve, hlo_done, n - 2)
                if e == 0:
                    nc.vector.tensor_tensor(h[e % 3][:, :], silu[k][:, :], b_bank[k][:, :], ALU.mult).then_inc(prod_done, 1)
                    return
                gated = c * EXPERTS + e - 1
                wait_count(dve, h_done, gated)
                nc.vector.tensor_tensor(prod[:, :], silu[k][:, :], b_bank[k][:, :], ALU.mult).then_inc(prod_done, 1)
                dve.wait_ge(prod_done, n + 1)
                dve.wait_ge(gate_b_done, gated + 1)
                nc.vector.tensor_tensor(h[e % 3][:, :], prod[:, :], gate_bank[:, :], ALU.mult).then_inc(h_done, 1)

            def residual(c):
                dve.wait_ge(y_tok_done, c + 1)
                nc.vector.tensor_tensor(x[:, bass.ds(c * TILES, TILES), :], x[:, bass.ds(c * TILES, TILES), :],
                                        t_bank[:, :].rearrange("p (t d) -> p t d", d=P), ALU.add).then_inc(x_added, 1)

            def chunk(c, slot):
                for e in range(STEPS):
                    swiglu(c, slot, e)
                    if e == 0 and not is_last(c):
                        split_x(c + 1, 1 - slot)
                    if e in (2, 3, 4, 5, 6) and not is_last(c):
                        gates(c + 1, e - 2)
                    if e == 5 and not is_first(c):
                        residual(c - 1)
                    if e == 6 and exists(c + 2):
                        norm(c + 2, slot)
                    if e == 7 and exists(c + 2):
                        scale(c + 2)

            norm(0, 0)
            scale(0)
            split_x(0, 0)
            norm(1, 1)
            scale(1)
            for part in range(len(GATE_PARTS) - 1):
                gates(0, part)
            run_pairs(dve, chunk)
            residual(CHUNKS - 1)

        @block.tensor
        def _(pe):
            def turn_x(c):
                pe.wait_ge(ln_done, c + 1)
                wait_count(pe, x_added, c - 2)
                for t in range(TILES):
                    last = nc.tensor.transpose(t_bank[:, t * P:(t + 1) * P], xn[:, t, :], ident[:, :])
                last.then_inc(xt_done, 1)

            def router(c, slot):
                pe.wait_ge(xhi_done, c + 1)
                pe.wait_ge(xlo_done, c + 1)
                wait_count(pe, gate_t_done, c)
                for t in range(TILES):
                    tile = slice(t * P, (t + 1) * P)
                    pairs = ((xt_hi, w["router_hi"]), (xt_hi, w["router_lo"]), (xt_lo, w["router_hi"]))
                    for i, (xs, ws) in enumerate(pairs):
                        last = nc.tensor.matmul(logits[:, t, :], xs[slot][:, tile], ws[:, :],
                                                start=(i == 0), stop=(i == 2))
                last.then_inc(logits_done, 1)

            def turn_gates(c):
                pe.wait_ge(gates_done, c + 1)
                for t in range(TILES):
                    last = nc.tensor.transpose(gate_tp[:, t * P:(t + 1) * P], gate_parts[:, t, :],
                                               consts["ident16"][:, :])
                last.then_inc(gate_tp_done, 1)

            def up(c, slot, e):
                n, k = c * STEPS + e, (slot + e) % 2
                if e == 0:
                    pe.wait_ge(xhi_done, c + 1)
                    pe.wait_ge(xlo_done, c + 1)
                for dst, name, free, done in ((a_bank, "w1", silu_done, a_done), (b_bank, "w3", prod_done, b_done)):
                    wait_count(pe, free, n - 1)
                    pairs = ((w[name + "_hi"], xt_hi), (w[name + "_lo"], xt_hi), (w[name + "_hi"], xt_lo))
                    for i, (ws, xs) in enumerate(pairs):
                        last = nc.tensor.matmul(dst[k][:, :], ws[:, e, :], xs[slot][:, :], start=(i == 0), stop=(i == 2))
                    last.then_inc(done, 1)

            def spread_gate(c, slot, e):
                if e == 1:
                    pe.wait_ge(gate_t_done, c + 1)
                wait_count(pe, h_done, c * EXPERTS + e - 1)
                nc.tensor.matmul(gate_bank[:, :], select_gate[:, e - 1, :], gate_t[slot][:, :],
                                 start=True, stop=True).then_inc(gate_b_done, 1)

            def down(c, slot, e):
                n, k = c * STEPS + e, e % 3
                pe.wait_ge(hhi_done, n + 1)
                pe.wait_ge(hlo_done, n + 1)
                if e == 0:
                    wait_count(pe, yt_done, c)
                pairs = ((w["w2_hi"], h_hi), (w["w2_lo"], h_hi), (w["w2_hi"], h_lo))
                for i, (ws, hs) in enumerate(pairs):
                    last = nc.tensor.matmul(y_bank[:, :], ws[:, e, :], hs[k][:, :],
                                            start=(e == 0 and i == 0), stop=(e == STEPS - 1 and i == 2))
                last.then_inc(w2_done, 1)

            def turn_y(c):
                pe.wait_ge(yt_done, c + 1)
                pe.wait_ge(xlo_done, min(c + 2, CHUNKS) if isinstance(c, int) else c + 2)
                for t in range(TILES):
                    last = nc.tensor.transpose(t_bank[:, t * P:(t + 1) * P], yt[:, t * P:(t + 1) * P], ident[:, :])
                last.then_inc(y_tok_done, 1)

            def chunk(c, slot):
                for e in range(STEPS):
                    up(c, slot, e)
                    if e > 0:
                        spread_gate(c, slot, e)
                    if e == 0 and not is_last(c):
                        turn_x(c + 1)
                    if e >= LAG:
                        down(c, slot, e - LAG)
                    elif not is_first(c):
                        down(c - 1, 1 - slot, STEPS - LAG + e)
                    if e == 1 and not is_last(c):
                        router(c + 1, 1 - slot)
                    if e == 4 and not is_first(c):
                        turn_y(c - 1)
                    if e == 7 and not is_last(c):
                        turn_gates(c + 1)

            turn_x(0)
            router(0, 0)
            turn_gates(0)
            run_pairs(pe, chunk)
            for e in range(STEPS - LAG, STEPS):
                down(CHUNKS - 1, 1, e)
            turn_y(CHUNKS - 1)

        @block.scalar
        def _(act):
            def split_x(c, slot):
                act.wait_ge(xt_done, c + 1)
                wait_count(act, b_done, (c - 1) * STEPS)
                nc.scalar.activation(xt_hi[slot][:, :], t_bank[:, :], ACT.Copy).then_inc(xhi_done, 1)

            def expd(c):
                act.wait_ge(gate_step, c * GATE_STEPS + GATE_PARTS[1])
                nc.scalar.activation(g["expd"][:, :, :], g["shifted"][:, :, :], ACT.Exp).then_inc(expd_done, 1)

            def take_gates(c, slot):
                act.wait_ge(gate_tp_done, c + 1)
                wait_count(act, gate_b_done, (c - 1) * EXPERTS)
                nc.scalar.activation(gate_t[slot][:, :], gate_tp, ACT.Copy).then_inc(gate_t_done, 1)

            def silu_a(c, slot, e):
                n, k = c * STEPS + e, (slot + e) % 2
                act.wait_ge(a_done, n + 1)
                wait_count(act, prod_done, n - 1)
                nc.scalar.activation(silu[k][:, :], a_bank[k][:, :], ACT.Silu).then_inc(silu_done, 1)

            def split_h(c, slot, e):
                n, k = c * STEPS + e, e % 3
                if e == 0:
                    act.wait_ge(prod_done, n + 1)
                else:
                    act.wait_ge(h_done, c * EXPERTS + e)
                wait_count(act, w2_done, n - 2)
                wait_count(act, hlo_done, n - 2)
                nc.scalar.activation(h_hi[k][:, :], h[k][:, :], ACT.Copy).then_inc(hhi_done, 1)

            def take_y(c):
                act.wait_ge(w2_done, (c + 1) * STEPS)
                wait_count(act, y_tok_done, c)
                nc.scalar.activation(yt[:, :], y_bank[:, :], ACT.Copy, scale=0.5).then_inc(yt_done, 1)

            def chunk(c, slot):
                for e in range(STEPS):
                    silu_a(c, slot, e)
                    if e == 0 and not is_last(c):
                        split_x(c + 1, 1 - slot)
                    if e > 0:
                        split_h(c, slot, e - 1)
                    elif not is_first(c):
                        split_h(c - 1, 1 - slot, STEPS - 1)
                    if e == 3 and not is_first(c):
                        take_y(c - 1)
                    if e == 3 and not is_last(c):
                        expd(c + 1)
                    if e == 8 and not is_last(c):
                        take_gates(c + 1, 1 - slot)

            split_x(0, 0)
            expd(0)
            take_gates(0, 0)
            run_pairs(act, chunk)
            split_h(CHUNKS - 1, 1, STEPS - 1)
            take_y(CHUNKS - 1)

        @block.gpsimd
        def _(pool):
            def low_part(c, e):
                n, k = c * STEPS + e, e % 3
                pool.wait_ge(hhi_done, n + 1)
                wait_count(pool, w2_done, n - 2)
                nc.gpsimd.tensor_tensor(h_lo[k][:, :], h[k][:, :], h_hi[k][:, :], ALU.subtract).then_inc(hlo_done, 1)

            def chunk(c, slot):
                for e in range(STEPS):
                    low_part(c, e)
                    if e == 5 and exists(c + 2):
                        norm_root(pool, nc, c + 2, buf, ln_step, ln_rooted)

            norm_root(pool, nc, 0, buf, ln_step, ln_rooted)
            norm_root(pool, nc, 1, buf, ln_step, ln_rooted)
            run_pairs(pool, chunk)




def split_weights(nc, consts, w, ffn, attn, bias, router):
    with ExitStack() as ctx:
        def sb(name, shape, dt):
            return ctx.enter_context(nc.sbuf_tensor(name, shape, dt))

        def sem(name):
            return ctx.enter_context(nc.semaphore(name))

        raw = {n: sb(f"raw_{n}", [P, STEPS, P], F32) for n in ("w1", "w3", "w2")}
        raw_router = sb("raw_router", [P, EXPERTS], F32)
        raw_attn = {n: sb(f"raw_{n}", [P, P], F32) for n in attn}
        turned_bank = ctx.enter_context(nc.psum_tensor("turned_bank", [P, 4 * P], F32))
        zeros = sb("zeros", [P, P], F32)
        loaded, zeroed, ident_done = sem("w_loaded"), sem("zeroed"), sem("ident_done")
        hi_done, lo_done, turned, tables = sem("w_hi_done"), sem("w_lo_done"), sem("w_turned"), sem("tables")
        loads = 6 + 2 + len(attn)
        names = ("w1", "w3", "w2")
        block = ctx.enter_context(nc.Block())

        @block.sync
        def _(sp):
            for n in names:
                shared, routed = ffn[n]
                sp.dma_start(raw[n][:, 0, :], shared).then_inc(loaded, DMA)
                sp.dma_start(raw[n][:, 1:STEPS, :], routed.rearrange("e d h -> d e h")).then_inc(loaded, DMA)
            sp.dma_start(raw_router[:, :], router).then_inc(loaded, DMA)
            sp.dma_start(consts["bias"][:, :], bias.rearrange("(a e) -> a e", a=1).to_broadcast([P, EXPERTS])
                         ).then_inc(loaded, DMA)
            for n in attn:
                sp.dma_start(raw_attn[n][:, :], attn[n]).then_inc(loaded, DMA)
            sp.wait_ge(loaded, loads * DMA)

        @block.gpsimd
        def _(pool):
            nc.gpsimd.memset(zeros[:, :], 0.0).then_inc(zeroed, 1)
            pool.wait_ge(zeroed, 1)
            nc.gpsimd.affine_select(out=consts["ident"][:, :], in_=zeros[:, :], compare_op=ALU.not_equal, fill=1.0,
                                    base=0, pattern=[[-1, P]], channel_multiplier=1).then_inc(ident_done, 1)
            nc.gpsimd.affine_select(out=consts["causal"][:, :], in_=zeros[:, :], compare_op=ALU.is_ge, fill=-FAR,
                                    base=0, pattern=[[-1, P]], channel_multiplier=1).then_inc(tables, 1)
            nc.gpsimd.memset(consts["eps"][:, :], LN_EPS).then_inc(tables, 1)
            nc.gpsimd.memset(consts["power"][:, :], -0.5).then_inc(tables, 1)
            for e in range(EXPERTS):
                nc.gpsimd.memset(consts["order"][:, e:e + 1], float(EXPERTS - e)).then_inc(tables, 1)

        @block.tensor
        def _(pe):
            pe.wait_ge(loaded, loads * DMA)
            pe.wait_ge(ident_done, 1)
            for i, n in enumerate(attn):
                last = nc.tensor.transpose(turned_bank[:, i * P:(i + 1) * P], raw_attn[n][:, :], consts["ident"][:, :])
            last.then_inc(turned, 1)

        @block.scalar
        def _(act):
            act.wait_ge(loaded, loads * DMA)
            for n in names:
                nc.scalar.activation(w[n + "_hi"][:, :, :], raw[n][:, :, :], ACT.Copy).then_inc(hi_done, 1)
            nc.scalar.activation(w["router_hi"][:, :], raw_router[:, :], ACT.Copy).then_inc(hi_done, 1)
            act.wait_ge(turned, 1)
            nc.scalar.activation(w["attn_hi"][:, :, :], turned_bank[:, :].rearrange("p (i n) -> p i n", n=P),
                                 ACT.Copy).then_inc(hi_done, 1)

        @block.vector
        def _(dve):
            dve.wait_ge(ident_done, 1)
            ident = consts["ident"]
            nc.vector.tensor_copy(consts["ident16"][:, :], ident[:, :]).then_inc(tables, 1)
            nc.vector.tensor_copy(consts["ident_b"][:, :], ident[:, :]).then_inc(tables, 1)
            K = 2 * EXPERTS
            nc.vector.tensor_tensor(consts["select_gate"][:, :, :],
                                    ident[0:K, 0:EXPERTS].unsqueeze(2).to_broadcast([K, EXPERTS, P]),
                                    ident[0:K, EXPERTS:K].unsqueeze(2).to_broadcast([K, EXPERTS, P]),
                                    ALU.add).then_inc(tables, 1)
            for i, n in enumerate(names):
                dve.wait_ge(hi_done, i + 1)
                nc.vector.tensor_tensor(w[n + "_lo"][:, :, :], raw[n][:, :, :], w[n + "_hi"][:, :, :],
                                        ALU.subtract).then_inc(lo_done, 1)
            dve.wait_ge(hi_done, 4)
            nc.vector.tensor_tensor(w["router_lo"][:, :], raw_router[:, :], w["router_hi"][:, :],
                                    ALU.subtract).then_inc(lo_done, 1)
            dve.wait_ge(hi_done, 5)
            nc.vector.tensor_tensor(w["attn_lo"][:, :, :], turned_bank[:, :].rearrange("p (i n) -> p i n", n=P),
                                    w["attn_hi"][:, :, :], ALU.subtract).then_inc(lo_done, 1)
            select_heads(nc, consts, tables)


def select_heads(nc, consts, tables):
    ident = consts["ident"][:, :].rearrange("p (g j d) -> p g j d", g=GROUPS, j=UNITS)
    for name, places in (("sel_q_hi", (0, 1)), ("sel_q_lo", (2,)), ("sel_k_hi", (0, 2)), ("sel_k_lo", (1,))):
        table = consts[name][:, :, :].rearrange("p g (j r) -> p g j r", r=ROWS)
        for place in range(ROWS // HEAD):
            dst = table[:, :, :, place * HEAD:(place + 1) * HEAD]
            if place in places:
                nc.vector.tensor_copy(dst, ident).then_inc(tables, 1)
            else:
                nc.vector.tensor_scalar(dst, ident, 0.0, None, ALU.mult).then_inc(tables, 1)
    nc.vector.tensor_reduce(consts["max_row"][:, :], consts["ident"][:, MAX_ROW:P:ROWS], AX.X,
                            ALU.add).then_inc(tables, 1)


JOBS = ["q", "k", "o10", "o11", "Q00", "K00", "y1", "Q01", "K01", "z1", "m10", "m11",
        "Q10", "K10", "o00", "o01", "Q11", "K11", "y0", "v", "z0", "x", "m00", "m01"]
SHIFT = {n: -2 if n == "x" else -1 if n in ("m00", "m01") or n[0] in "qkQKv" else 1 if n in ("o10", "o11", "y1", "z1")
         else 0 for n in JOBS}


def jobs_of(turn):
    return [n for n in JOBS if exists(turn - SHIFT[n])]


def job_at(c, name):
    if isinstance(c, int):
        turn = c + SHIFT[name]
        n = sum(len(jobs_of(t)) for t in range(-2, turn)) + jobs_of(turn).index(name)
        return n % 2, n // 2
    n = sum(len(jobs_of(t)) for t in range(-2, 1)) + (SHIFT[name] - 1) * len(JOBS) + JOBS.index(name)
    return n % 2, c * (len(JOBS) // 2) + n // 2


JOBS_BEHIND = ((("q", "k"), ("o10", "o11", "Q00", "K00"), ("y1", "Q01", "K01"), ("z1",)),
               (("Q10", "K10"), ("o00", "o01", "Q11", "K11"), ("y0", "v"), ("z0", "x")))


def attention_phase(nc, x, consts, w):
    with ExitStack() as ctx:
        def sb(name, shape, dt):
            return ctx.enter_context(nc.sbuf_tensor(f"{name}_at", shape, dt))

        def bank(name):
            return ctx.enter_context(nc.psum_tensor(f"{name}_at", [P, CHUNK], F32))

        def sem(name):
            return ctx.enter_context(nc.semaphore(f"{name}_at"))

        ident, ident16 = consts["ident"], consts["ident16"]
        buf = {
            "stats": sb("stats", [P, TILES, 6], F32), "moments": sb("moments", [P, TILES, 2], F32),
            "rstd": sb("rstd", [P, TILES], F32), "var_eps": sb("var_eps", [P, TILES], F32), "power": consts["power"],
            "eps": consts["eps"], "spare": sb("spare", [P, 1], F32),
            "xn": sb("xn", [P, TILES, P], F32),
        }
        xn = buf["xn"]
        xt_hi, xt_lo = sb("xt_hi", [P, CHUNK], F16), sb("xt_lo", [P, CHUNK], F16)
        part = {n: sb(n, [P, CHUNK], F16) for n in ("q_hi", "q_lo", "k_hi", "k_lo")}
        q_pack = [sb(f"q_pack{s}", [P, GROUPS, CHUNK], F16) for s in range(2)]
        k_pack = [sb(f"k_pack{s}", [P, GROUPS, CHUNK], F16) for s in range(2)]
        v_ones = [sb(f"v_ones{s}", [P, TILES, HEADS, ROWS], F32) for s in range(2)]
        neg_max = sb("neg_max", [P, 2, GROUPS, UNITS, ROWS], F16)
        probs = [sb(f"probs{s}", [P, 3, CHUNK], F32) for s in range(2)]
        o_t = [sb(f"o_t{s}", [P, UNITS, SEQ], F32) for s in range(2)]
        inv = sb("inv", [P, 2, UNITS, GROUPS], F32)
        y = sb("y", [P, 2, P], F32)
        yt_hi, yt_lo = sb("yt_hi", [P, SEQ], F16), sb("yt_lo", [P, SEQ], F16)

        score_bank = [bank(f"score{s}") for s in range(2)]
        prob_bank = [bank(f"prob{i}") for i in range(3)]
        o_bank = bank("o")
        job_bank = [bank(f"job{s}") for s in range(2)]

        job_written = [sem(f"job_written{s}") for s in range(2)]
        job_taken = [sem(f"job_taken{s}") for s in range(2)]
        ln_step, ln_rooted, ln_done, buffers_set = (sem(n) for n in ("ln_step", "ln_rooted", "ln_done", "buffers_set"))
        xhi_done, qkhi_done, yhi_done, inv_done = (sem(n) for n in ("xhi_done", "qkhi_done", "yhi_done", "inv_done"))
        mask_begun = sem("mask_begun")
        scored, max_done = sem("scored"), sem("max_done")
        st_done, exp_done, masked, pv_done, o_done = (
            sem(n) for n in ("st_done", "exp_done", "masked", "pv_done", "o_done"))

        block = ctx.enter_context(nc.Block())

        def take(eng, c, name):
            k, before = job_at(c, name)
            eng.wait_ge(job_written[k], before + 1)
            return job_bank[k], job_taken[k]

        def wait_taken(eng, c, name):
            k, before = job_at(c, name)
            eng.wait_ge(job_taken[k], before + 1)

        def packed(pack, name):
            b, half = int(name[1]), int(name[2])
            return pack[:, 2 * half:2 * half + 2, b * SEQ:(b + 1) * SEQ]

        def unit_rows(j):
            return slice(ROWS * j, ROWS * (j + 1))

        def turn_jobs(do, c, slot, names):
            for name in names:
                if exists(c - SHIFT[name]):
                    do(c - SHIFT[name], (slot - SHIFT[name]) % 2, name)

        @block.tensor
        def _(pe):
            def begin(c, name):
                k, before = job_at(c, name)
                wait_count(pe, job_taken[k], before)
                return job_bank[k], job_written[k]

            def product(dst, pairs):
                for n, (stationary, moving) in enumerate(pairs):
                    last = nc.tensor.matmul(dst, stationary, moving, start=(n == 0), stop=(n == 2))
                return last

            w_hi, w_lo = w["attn_hi"], w["attn_lo"]

            def job(c, slot, name):
                kind = name[0]
                if kind == "x":
                    pe.wait_ge(ln_done, c + 1)
                    dst, done = begin(c, name)
                    for t in range(TILES):
                        last = nc.tensor.transpose(dst[:, t * P:(t + 1) * P], xn[:, t, :], ident[:, :])
                elif kind in "qk":
                    wait_taken(pe, c, "x")
                    dst, done = begin(c, name)
                    i = "qk".index(kind)
                    last = product(dst[:, :], ((w_hi[:, i, :], xt_hi[:, :]), (w_lo[:, i, :], xt_hi[:, :]),
                                               (w_hi[:, i, :], xt_lo[:, :])))
                elif kind in "QK":
                    m, b, half = kind.lower(), int(name[1]), int(name[2])
                    wait_taken(pe, c, m)
                    dst, done = begin(c, name)
                    tokens = slice(b * SEQ, (b + 1) * SEQ)
                    for i in range(2):
                        tile = dst[:, i * SEQ:(i + 1) * SEQ]
                        nc.tensor.matmul(tile, consts[f"sel_{m}_hi"][:, 2 * half + i, :], part[m + "_hi"][:, tokens],
                                         start=True, stop=False)
                        last = nc.tensor.matmul(tile, consts[f"sel_{m}_lo"][:, 2 * half + i, :],
                                                part[m + "_lo"][:, tokens], start=False, stop=True)
                elif kind == "v":
                    dst, done = begin(c, name)
                    for t in range(TILES):
                        tile = slice(t * P, (t + 1) * P)
                        last = product(dst[:, tile], ((xt_hi[:, tile], w_hi[:, 2, :]), (xt_hi[:, tile], w_lo[:, 2, :]),
                                                      (xt_lo[:, tile], w_hi[:, 2, :])))
                elif kind == "o":
                    b, t = int(name[1]), int(name[2])
                    pe.wait_ge(o_done, c * 2 * UNITS + (b + 1) * UNITS)
                    dst, done = begin(c, name)
                    for j in range(UNITS):
                        last = nc.tensor.transpose(dst[:, j * P:(j + 1) * P], o_t[b][:, j, t * P:(t + 1) * P],
                                                   ident[:, :])
                elif kind == "y":
                    b = int(name[1])
                    wait_taken(pe, c, f"o{b}0")
                    wait_taken(pe, c, f"o{b}1")
                    dst, done = begin(c, name)
                    for t in range(2):
                        last = nc.tensor.transpose(dst[:, t * P:(t + 1) * P], y[:, t, :], ident[:, :])
                elif kind == "z":
                    wait_taken(pe, c, "y" + name[1])
                    dst, done = begin(c, name)
                    for t in range(2):
                        tile = slice(t * P, (t + 1) * P)
                        last = product(dst[:, tile], ((yt_hi[:, tile], w_hi[:, 3, :]), (yt_hi[:, tile], w_lo[:, 3, :]),
                                                      (yt_lo[:, tile], w_hi[:, 3, :])))
                elif kind == "m":
                    b, t = int(name[1]), int(name[2])
                    pe.wait_ge(max_done, c * 24 + (b + 1) * 12)
                    dst, done = begin(c, name)
                    for g in range(GROUPS):
                        last = nc.tensor.matmul(dst[:, g * P:(g + 1) * P],
                                                neg_max[:, t, g, :, :].rearrange("p j r -> p (j r)"), ident16[:, :],
                                                start=True, stop=True)
                last.then_inc(done, 1)

            def scores(c, slot, b, j):
                if j == 0:
                    wait_taken(pe, c, f"Q{b}1")
                    wait_taken(pe, c, f"K{b}1")
                rows, first = unit_rows(j), b * SEQ
                for i in range(3):
                    n = c * 24 + b * 12 + 3 * j + i
                    wait_count(pe, max_done, n - 1)
                    dst = score_bank[(3 * j + i) % 2]
                    groups = range(GROUPS) if i == 0 else range(2 * i - 2, 2 * i)
                    keys = P if i == 0 else SEQ
                    view = dst[:, :].rearrange("p (h k) -> p h k", k=keys)
                    nc.tensor.matmul(view[:, :, keys - P:keys], consts["ident_b"][:, :],
                                     consts["causal"][:, :].unsqueeze(1).to_broadcast([P, len(groups), P]),
                                     start=True, stop=False, skip_group_check=True)
                    q0 = first + (0 if i == 0 else P)
                    for h, g in enumerate(groups):
                        last = nc.tensor.matmul(view[:, h, :], q_pack[slot][rows, g, q0:q0 + P],
                                                k_pack[slot][rows, g, first:first + keys], start=False,
                                                stop=(h == len(groups) - 1), skip_group_check=True)
                    last.then_inc(scored, 1)

            def scores_t(c, slot, b, j):
                rows, first = unit_rows(j), b * SEQ
                unit = c * 2 * UNITS + b * UNITS + j
                if j == 0:
                    wait_taken(pe, c, f"m{b}0")
                    wait_taken(pe, c, f"m{b}1")
                for i in range(3):
                    wait_count(pe, exp_done, unit * 3 - 2 + i)
                    pe.wait_ge(buffers_set, 1)
                    keys = slice(first, first + P) if i < 2 else slice(first + P, first + SEQ)
                    queries = slice(keys.start, first + SEQ)
                    width = queries.stop - queries.start
                    for h, g in enumerate(range(2 * i, 2 * i + 2) if i < 2 else range(GROUPS)):
                        last = nc.tensor.matmul(prob_bank[i][:, h * width:(h + 1) * width],
                                                k_pack[slot][rows, g, keys], q_pack[slot][rows, g, queries],
                                                start=True, stop=True)
                    last.then_inc(st_done, 1)

            def weigh(c, slot, b, j):
                unit = c * 2 * UNITS + b * UNITS + j
                if j == 0 and b == 0:
                    wait_taken(pe, c, "v")
                pe.wait_ge(masked, unit * 2 + 2)
                wait_count(pe, o_done, unit)
                for t in range(2):
                    for g in range(GROUPS):
                        src = (probs[j % 2][:, g // 2, (g % 2) * SEQ:(g % 2 + 1) * SEQ] if t == 0
                               else probs[j % 2][:, 2, g * P:(g + 1) * P])
                        last = nc.tensor.matmul(o_bank[g * ROWS:(g + 1) * ROWS, t * P:SEQ],
                                                v_ones[slot][:, 2 * b + t, GROUPS * g + j, :], src,
                                                start=(t == 0), stop=(t == 1), skip_group_check=True)
                last.then_inc(pv_done, 1)

            def turn(c, slot):
                for b in range(2):
                    for j in range(UNITS):
                        scores_t(c, slot, b, j)
                        if b == 0:
                            scores(c, slot, 1, j)
                        elif exists(c + 1):
                            scores(c + 1, 1 - slot, 0, j)
                        if j > 0:
                            weigh(c, slot, b, j - 1)
                        elif b == 1:
                            weigh(c, slot, 0, UNITS - 1)
                        elif exists(c - 1):
                            weigh(c - 1, 1 - slot, 1, UNITS - 1)
                        turn_jobs(job, c, slot, JOBS_BEHIND[b][j])
                    turn_jobs(job, c, slot, ("m10", "m11") if b == 0 else ("m00", "m01"))

            turn_jobs(job, -2, 0, ("x",))
            turn_jobs(job, -1, 1, JOBS[:-3])
            turn_jobs(job, -1, 1, ("x",))
            for j in range(UNITS):
                scores(0, 0, 0, j)
            turn_jobs(job, -1, 1, ("m00", "m01"))
            run_pairs(pe, turn)
            weigh(CHUNKS - 1, 1, 1, UNITS - 1)
            turn_jobs(job, CHUNKS, 0, JOBS)

        @block.vector
        def _(dve):
            def norm(c):
                norm_stats(dve, nc, c, x, buf, ln_step, ln_done)

            def scale(c):
                if not is_first(c):
                    wait_taken(dve, c - 1, "x")
                norm_scale(dve, nc, c, x, buf, ln_rooted, ln_done)

            def job(c, slot, name):
                kind = name[0]
                if kind in "Kv":
                    return
                src, done = take(dve, c, name)
                if kind == "x":
                    dve.wait_ge(xhi_done, c + 1)
                    last = nc.vector.tensor_tensor(xt_lo[:, :], src[:, :], xt_hi[:, :], ALU.subtract)
                elif kind in "qk":
                    dve.wait_ge(qkhi_done, c * 2 + (1 if kind == "q" else 2))
                    last = nc.vector.tensor_tensor(part[kind + "_lo"][:, :], src[:, :], part[kind + "_hi"][:, :],
                                                   ALU.subtract)
                elif kind == "Q":
                    wait_count(dve, st_done, (c - 1) * 6 * UNITS)
                    last = nc.vector.tensor_copy(packed(q_pack[slot], name),
                                                 src[:, :].rearrange("p (g n) -> p g n", n=SEQ))
                elif kind == "m":
                    first = int(name[1]) * SEQ + int(name[2]) * P
                    q = q_pack[slot][:, :, first:first + P]
                    last = nc.vector.tensor_tensor(q, src[:, :].rearrange("p (g q) -> p g q", q=P), q, ALU.add)
                elif kind == "o":
                    b, t = int(name[1]), int(name[2])
                    o = src[:, :].rearrange("p (j g r) -> p j g r", j=UNITS, r=ROWS)
                    nc.vector.reciprocal(inv[:, t, :, :], o[:, :, :, HEAD]).then_inc(inv_done, 1)
                    dve.wait_ge(inv_done, c * 4 + 2 * b + t + 1)
                    last = nc.vector.tensor_tensor(y[:, t, :].rearrange("p (g j d) -> p j g d", j=UNITS, d=HEAD),
                                                   o[:, :, :, 0:HEAD],
                                                   inv[:, t, :, :].unsqueeze(3).to_broadcast([P, UNITS, GROUPS, HEAD]),
                                                   ALU.mult)
                elif kind == "y":
                    dve.wait_ge(yhi_done, c * 2 + int(name[1]) + 1)
                    last = nc.vector.tensor_tensor(yt_lo[:, :], src[:, 0:SEQ], yt_hi[:, :], ALU.subtract)
                elif kind == "z":
                    rows = x[:, bass.ds(c * TILES + 2 * int(name[1]), 2), :]
                    last = nc.vector.tensor_tensor(rows, rows, src[:, 0:SEQ].rearrange("p (t d) -> p t d", d=P),
                                                   ALU.add)
                last.then_inc(done, 1)

            def maxima(c, b, j):
                for i in range(3):
                    n = c * 24 + b * 12 + 3 * j + i
                    dve.wait_ge(scored, n + 1)
                    src = score_bank[(3 * j + i) % 2][:, :].rearrange("p (h k) -> p h k", k=P if i == 0 else SEQ)
                    dst = (neg_max[:, 0, :, j, MAX_ROW] if i == 0 else neg_max[:, 1, 2 * i - 2:2 * i, j, MAX_ROW])
                    nc.vector.tensor_reduce(dst, src, AX.X, ALU.max, negate=True).then_inc(max_done, 1)

            def turn(c, slot):
                for b in range(2):
                    for j in range(UNITS):
                        if b == 0:
                            maxima(c, 1, j)
                        elif exists(c + 1):
                            maxima(c + 1, 0, j)
                        if b == 1 and j == 1 and exists(c + 2):
                            norm(c + 2)
                        if b == 1 and j == 2 and exists(c + 2):
                            scale(c + 2)
                        turn_jobs(job, c, slot, JOBS_BEHIND[b][j])
                    turn_jobs(job, c, slot, ("m10", "m11") if b == 0 else ("m00", "m01"))

            nc.vector.memset(neg_max[:, :, :, :, :].rearrange("p a b c d -> p (a b c d)"), 0.0)
            for s in range(2):
                v = v_ones[s][:, :, :, :].rearrange("p t h r -> p (t h) r")
                nc.vector.memset(v[:, :, HEAD + 1:ROWS], 0.0)
                last = nc.vector.memset(v[:, :, HEAD:HEAD + 1], 1.0)
            last.then_inc(buffers_set, 1)
            norm(0)
            scale(0)
            turn_jobs(job, -2, 0, ("x",))
            turn_jobs(job, -1, 1, JOBS[:-3])
            norm(1)
            scale(1)
            turn_jobs(job, -1, 1, ("x",))
            dve.wait_ge(buffers_set, 1)
            for j in range(UNITS):
                maxima(0, 0, j)
            turn_jobs(job, -1, 1, ("m00", "m01"))
            run_pairs(dve, turn)
            turn_jobs(job, CHUNKS, 0, JOBS)

        @block.scalar
        def _(act):
            def job(c, slot, name):
                kind = name[0]
                if kind in "Qmoz":
                    return
                if kind == "y":
                    b = int(name[1])
                    if b == 1:
                        wait_taken(act, c, "z0")
                    elif not is_first(c):
                        wait_taken(act, c - 1, "z1")
                src, done = take(act, c, name)
                if kind == "x":
                    nc.scalar.activation(xt_hi[:, :], src[:, :], ACT.Copy).then_inc(xhi_done, 1)
                elif kind in "qk":
                    nc.scalar.activation(part[kind + "_hi"][:, :], src[:, :], ACT.Copy).then_inc(qkhi_done, 1)
                elif kind == "K":
                    nc.scalar.activation(packed(k_pack[slot], name), src[:, :].rearrange("p (g n) -> p g n", n=SEQ),
                                         ACT.Identity, bias=consts["max_row"][:, :]).then_inc(done, 1)
                elif kind == "v":
                    nc.scalar.activation(v_ones[slot][:, :, :, 0:HEAD],
                                         src[:, :].rearrange("p (t h d) -> p t h d", t=TILES, d=HEAD),
                                         ACT.Copy).then_inc(done, 1)
                elif kind == "y":
                    nc.scalar.activation(yt_hi[:, :], src[:, 0:SEQ], ACT.Copy).then_inc(yhi_done, 1)

            def exponents(c, b, j):
                unit = c * 2 * UNITS + b * UNITS + j
                for i in range(3):
                    act.wait_ge(st_done, unit * 3 + i + 1)
                    if i == 0:
                        wait_count(act, pv_done, unit - 1)
                    nc.scalar.activation(probs[j % 2][:, i, :], prob_bank[i][:, :], ACT.Exp,
                                         scale=SCALE).then_inc(exp_done, 1)

            def take_o(c, b, j):
                unit = c * 2 * UNITS + b * UNITS + j
                act.wait_ge(pv_done, unit + 1)
                nc.scalar.activation(o_t[b][:, j, :], o_bank[:, 0:SEQ], ACT.Copy).then_inc(o_done, 1)

            def turn(c, slot):
                for b in range(2):
                    for j in range(UNITS):
                        exponents(c, b, j)
                        if j > 0:
                            take_o(c, b, j - 1)
                        elif b == 1:
                            take_o(c, 0, UNITS - 1)
                        elif exists(c - 1):
                            take_o(c - 1, 1, UNITS - 1)
                        turn_jobs(job, c, slot, JOBS_BEHIND[b][j])

            act.wait_ge(buffers_set, 1)
            turn_jobs(job, -2, 0, ("x",))
            turn_jobs(job, -1, 1, JOBS[:-3])
            turn_jobs(job, -1, 1, ("x",))
            run_pairs(act, turn)
            take_o(CHUNKS - 1, 1, UNITS - 1)
            turn_jobs(job, CHUNKS, 0, JOBS)

        @block.gpsimd
        def _(pool):
            def mask(c, b, j):
                unit = c * 2 * UNITS + b * UNITS + j
                for i in range(2):
                    pool.wait_ge(exp_done, unit * 3 + 2 + i)
                    pool.sem_inc(mask_begun, 1)
                    p = (probs[j % 2][:, 0:2, :].rearrange("p i (h q) -> p (i h) q", q=SEQ)[:, :, 0:P] if i == 0
                         else probs[j % 2][:, 2, :].rearrange("p (h q) -> p h q", q=P))
                    nc.gpsimd.affine_select(out=p, in_=p, compare_op=ALU.is_ge, fill=0.0, base=0,
                                            pattern=[[0, GROUPS], [1, P]], channel_multiplier=-1).then_inc(masked, 1)

            def turn(c, slot):
                for b in range(2):
                    for j in range(UNITS):
                        mask(c, b, j)
                        if b == 1 and j == 1 and exists(c + 2):
                            norm_root(pool, nc, c + 2, buf, ln_step, ln_rooted)

            norm_root(pool, nc, 0, buf, ln_step, ln_rooted)
            norm_root(pool, nc, 1, buf, ln_step, ln_rooted)
            run_pairs(pool, turn)



def macaron_kernel(nc, L0_attn_x, L0_attn_W_Q, L0_attn_W_K, L0_attn_W_V, L0_attn_W_O, L0_ffn_router_w,
                   L0_ffn_expert_bias, L0_ffn_w1, L0_ffn_w2, L0_ffn_w3, L0_ffn_sw1, L0_ffn_sw2, L0_ffn_sw3, out):
    with ExitStack() as ctx:
        def sb(name, shape, dt):
            return ctx.enter_context(nc.sbuf_tensor(name, shape, dt))

        x = sb("x", [P, CHUNKS * TILES, P], F32)
        consts = {
            "ident": sb("ident", [P, P], F32), "ident16": sb("ident16", [P, P], F16),
            "ident_b": sb("ident_b", [P, P], BF16), "causal": sb("causal", [P, P], BF16),
            "bias": sb("bias", [P, EXPERTS], F32), "order": sb("order", [P, EXPERTS], F32),
            "power": sb("power", [P, TILES], F32), "eps": sb("eps", [P, TILES], F32),
            "max_row": sb("max_row", [P, 1], F32),
            "select_gate": sb("select_gate", [2 * EXPERTS, EXPERTS, P], F16),
        }
        for n in ("sel_q_hi", "sel_q_lo", "sel_k_hi", "sel_k_lo"):
            consts[n] = sb(n, [P, GROUPS, P], F16)
        w = {f"{n}_{part}": sb(f"{n}_{part}", [P, STEPS, P], F16)
             for n in ("w1", "w3", "w2") for part in ("hi", "lo")}
        for part in ("hi", "lo"):
            w["router_" + part] = sb("router_" + part, [P, EXPERTS], F16)
            w["attn_" + part] = sb("attn_" + part, [P, 4, P], F16)
        ffn = {"w1": (L0_ffn_sw1, L0_ffn_w1), "w3": (L0_ffn_sw3, L0_ffn_w3), "w2": (L0_ffn_sw2, L0_ffn_w2)}
        attn = {"wq": L0_attn_W_Q, "wk": L0_attn_W_K, "wv": L0_attn_W_V, "wo": L0_attn_W_O}
        x_dram = L0_attn_x.rearrange("b s d -> (b s) d")
        out_dram = out.rearrange("b s d -> (b s) d")

        split_weights(nc, consts, w, ffn, attn, L0_ffn_expert_bias, L0_ffn_router_w)
        ffn_phase(nc, x, consts, w, 0, x_dram, None)
        attention_phase(nc, x, consts, w)
        ffn_phase(nc, x, consts, w, 1, None, out_dram)


_INS = ['L0_attn_x', 'L0_attn_W_Q', 'L0_attn_W_K', 'L0_attn_W_V', 'L0_attn_W_O', 'L0_ffn_router_w',
        'L0_ffn_expert_bias', 'L0_ffn_w1', 'L0_ffn_w2', 'L0_ffn_w3', 'L0_ffn_sw1', 'L0_ffn_sw2', 'L0_ffn_sw3']
_OUTS = [((32, 256, 128), 'float32')]


def kernel(**inputs):
    import numpy as _np
    import concourse.bacc as _bacc
    from concourse import mybir as _mybir
    from concourse.bass_utils import run_bass_kernel_spmd as _run

    nc = _bacc.Bacc("TRN2", target_bir_lowering=False, num_devices=1)
    arrays, args = {}, []
    for name in _INS:
        a = _np.ascontiguousarray(inputs[name])
        arrays[f"in_{name}_dram"] = a
        args.append(nc.dram_tensor(f"in_{name}_dram", a.shape, _mybir.dt.from_np(a.dtype), kind="ExternalInput").ap())
    for i, (shape, dtype) in enumerate(_OUTS):
        dt = _mybir.dt.from_np(_np.dtype(dtype))
        args.append(nc.dram_tensor(f"out_{i}_dram", shape, dt, kind="ExternalOutput").ap())
    macaron_kernel(nc, *args)
    r = _run(nc, [arrays], core_ids=[0])
    got = tuple(r.results[0][f"out_{i}_dram"] for i in range(len(_OUTS)))
    return got[0]
```

```python
from contextlib import ExitStack

import concourse.bass as bass
from concourse import mybir

ALU = mybir.AluOpType
ACT = mybir.ActivationFunctionType
AX = mybir.AxisListType
F32 = mybir.dt.float32
F16 = mybir.dt.float16
BF16 = mybir.dt.bfloat16

P = 128
SEQ = 256
TILES = 4
CHUNK = TILES * P
CHUNKS = 32 * SEQ // CHUNK
EXPERTS = 8
STEPS = EXPERTS + 1
LAG = 3
LN_EPS = 1e-5
HEADS = 16
HEAD = P // HEADS
GROUPS = 4
ROWS = P // GROUPS
MAX_ROW = 3 * HEAD
SCALE = float(HEAD) ** -0.5
UNITS = 4
FAR = 1e30
GATE_PLACES = (0, 0, 0, 0, 0, 1, 2, 2, 2, 4, 6, 8, 10, 12, 14, 16, 18, 20, 21)
GATE_STEPS = GATE_PLACES[-1]
DMA = 16


def run_pairs(eng, chunk):
    chunk(0, 0)
    chunk(1, 1)
    with eng.Fori(1, CHUNKS // 2 - 1) as pair:
        chunk(pair * 2, 0)
        chunk(pair * 2 + 1, 1)
    chunk(CHUNKS - 2, 0)
    chunk(CHUNKS - 1, 1)


def is_first(c):
    return isinstance(c, int) and c == 0


def is_last(c):
    return isinstance(c, int) and c == CHUNKS - 1


def exists(c):
    return not isinstance(c, int) or 0 <= c < CHUNKS


def wait_count(eng, sem, value):
    if not isinstance(value, int) or value > 0:
        eng.wait_ge(sem, value)


LN_STEPS = 2 * TILES


def norm_stats(dve, nc, c, x, buf, step, scaled):
    base = c * LN_STEPS
    wait_count(dve, scaled, c)
    for t in range(TILES):
        nc.vector.bn_stats(buf["stats"][:, t, :], x[:, c * TILES + t, :]).then_inc(step, 1)
    dve.wait_ge(step, base + TILES)
    nc.vector.memset(buf["spare"][:, :], 0.0)
    for t in range(TILES):
        nc.vector.bn_aggr(buf["moments"][:, t, :], buf["stats"][:, t, :]).then_inc(step, 1)


def norm_root(pool, nc, c, buf, step, rooted):
    pool.wait_ge(step, (c + 1) * LN_STEPS)
    nc.gpsimd.tensor_tensor(buf["var_eps"][:, :], buf["moments"][:, :, 1], buf["eps"][:, :], ALU.add).then_inc(rooted, 1)
    pool.wait_ge(rooted, 2 * c + 1)
    nc.gpsimd.tensor_tensor(buf["rstd"][:, :], buf["var_eps"][:, :], buf["power"][:, :], ALU.pow).then_inc(rooted, 1)


def norm_scale(dve, nc, c, x, buf, rooted, scaled):
    dve.wait_ge(rooted, 2 * c + 2)
    for t in range(TILES):
        last = nc.vector.tensor_scalar(buf["xn"][:, t, :], x[:, c * TILES + t, :], buf["moments"][:, t, 0:1],
                                       buf["rstd"][:, t:t + 1], ALU.subtract, ALU.mult)
    last.then_inc(scaled, 1)


def ffn_phase(nc, x, consts, w, phase, x_dram, out):
    with ExitStack() as ctx:
        def sb(name, shape, dt):
            return ctx.enter_context(nc.sbuf_tensor(f"{name}_{phase}", shape, dt))

        def bank(name):
            return ctx.enter_context(nc.psum_tensor(f"{name}_{phase}", [P, CHUNK], F32))

        def sem(name):
            return ctx.enter_context(nc.semaphore(f"{name}_{phase}"))

        ident, select_gate = consts["ident"], consts["select_gate"]
        buf = {
            "stats": sb("stats", [P, TILES, 6], F32), "moments": sb("moments", [P, TILES, 2], F32),
            "rstd": sb("rstd", [P, TILES], F32), "var_eps": sb("var_eps", [P, TILES], F32), "power": consts["power"],
            "eps": consts["eps"], "spare": sb("spare", [P, 1], F32),
            "xn": sb("xn", [P, TILES, P], F32),
        }
        xn = buf["xn"]
        xt_hi = [sb(f"xt_hi{s}", [P, CHUNK], F16) for s in range(2)]
        xt_lo = [sb(f"xt_lo{s}", [P, CHUNK], F16) for s in range(2)]
        silu = [sb(f"silu{s}", [P, CHUNK], F32) for s in range(2)]
        prod = sb("prod", [P, CHUNK], F32)
        h = [sb(f"h{s}", [P, CHUNK], F32) for s in range(3)]
        h_hi = [sb(f"h_hi{s}", [P, CHUNK], F16) for s in range(3)]
        h_lo = [sb(f"h_lo{s}", [P, CHUNK], F16) for s in range(3)]
        yt = sb("yt", [P, CHUNK], F32)
        gate_t = [sb(f"gate_t{s}", [2 * EXPERTS, CHUNK], F16) for s in range(2)]
        g = {n: sb(n, [P, TILES, EXPERTS], F32) for n in
             ("shifted", "expd", "score", "biased", "hit", "rank", "first", "rest", "second", "gate")}
        top = {n: sb(n, [P, TILES], F32) for n in ("peak", "total", "inverse", "best1", "who1", "best2", "who2")}
        gate_parts = sb("gate_parts", [P, TILES, 2 * EXPERTS], F16)

        a_bank = [bank(f"a{s}") for s in range(2)]
        b_bank = [bank(f"b{s}") for s in range(2)]
        gate_bank, y_bank, t_bank, r_bank = bank("gate_b"), bank("y_b"), bank("t_b"), bank("r_b")
        logits = r_bank[:, 0:TILES * EXPERTS].rearrange("p (t e) -> p t e", e=EXPERTS)
        gate_tp = r_bank[0:2 * EXPERTS, 256:512].bitcast(F16)

        ln_rooted = sem("ln_rooted")
        x_loaded = [sem(f"x_loaded{s}") for s in range(2)]
        ln_step, ln_done, xt_done, xhi_done, xlo_done = (
            sem(n) for n in ("ln_step", "ln_done", "xt_done", "xhi_done", "xlo_done"))
        logits_done, gate_step, expd_done, gate_tp_done, gate_t_done = (
            sem(n) for n in ("logits_done", "gate_step", "expd_done", "gate_tp_done", "gate_t_done"))
        a_done, b_done, silu_done, prod_done, gate_b_done, h_done = (
            sem(n) for n in ("a_done", "b_done", "silu_done", "prod_done", "gate_b_done", "h_done"))
        hhi_done, hlo_done, w2_done, yt_done, y_tok_done, x_added, stored = (
            sem(n) for n in ("hhi_done", "hlo_done", "w2_done", "yt_done", "y_tok_done", "x_added", "stored"))

        block = ctx.enter_context(nc.Block())

        @block.sync
        def _(sp):
            if x_dram is not None:
                src = x_dram.rearrange("(c p) d -> p c d", p=P)
                for c in range(CHUNKS):
                    wait_count(sp, x_loaded[c % 2], c // 2 * DMA)
                    sp.dma_start(x[:, c * TILES:(c + 1) * TILES, :],
                                 src[:, c * TILES:(c + 1) * TILES, :]).then_inc(x_loaded[c % 2], DMA)
            if out is not None:
                dst = out.rearrange("(c p) d -> p c d", p=P)
                with sp.Fori(0, CHUNKS) as c:
                    sp.wait_ge(x_added, c + 1)
                    sp.dma_start(dst[:, bass.ds(c * TILES, TILES), :],
                                 x[:, bass.ds(c * TILES, TILES), :]).then_inc(stored, DMA)
                sp.wait_ge(stored, CHUNKS * DMA)

        @block.vector
        def _(dve):
            def norm(c, slot):
                if x_dram is not None:
                    dve.wait_ge(x_loaded[slot], ((c - slot) // 2 + 1) * DMA if isinstance(c, int)
                                else (c - slot) * (DMA // 2) + DMA)
                norm_stats(dve, nc, c, x, buf, ln_step, ln_done)

            def scale(c):
                wait_count(dve, xt_done, c)
                norm_scale(dve, nc, c, x, buf, ln_rooted, ln_done)

            def split_x(c, slot):
                dve.wait_ge(xhi_done, c + 1)
                nc.vector.tensor_tensor(xt_lo[slot][:, :], t_bank[:, :], xt_hi[slot][:, :],
                                        ALU.subtract).then_inc(xlo_done, 1)

            def gates(c, first, last):
                def wide(v):
                    return v[:, :].unsqueeze(2).to_broadcast([P, TILES, EXPERTS])

                bias = consts["bias"][:, :].unsqueeze(1).to_broadcast([P, TILES, EXPERTS])
                order = consts["order"][:, :].unsqueeze(1).to_broadcast([P, TILES, EXPERTS])
                for step in range(first, last):
                    if step == 0:
                        dve.wait_ge(logits_done, c + 1)
                    elif step == 2:
                        dve.wait_ge(expd_done, c + 1)
                    else:
                        dve.wait_ge(gate_step, c * GATE_STEPS + step)
                    if step == 0:
                        done = nc.vector.tensor_reduce(top["peak"][:, :], logits, AX.X, ALU.max)
                    elif step == 1:
                        done = nc.vector.tensor_tensor(g["shifted"][:, :, :], logits, wide(top["peak"]), ALU.subtract)
                    elif step == 2:
                        done = nc.vector.tensor_reduce(top["total"][:, :], g["expd"][:, :, :], AX.X, ALU.add)
                    elif step == 3:
                        done = nc.vector.reciprocal(top["inverse"][:, :], top["total"][:, :])
                    elif step == 4:
                        done = nc.vector.tensor_tensor(g["score"][:, :, :], g["expd"][:, :, :], wide(top["inverse"]),
                                                       ALU.mult)
                    elif step == 5:
                        done = nc.vector.tensor_tensor(g["biased"][:, :, :], g["score"][:, :, :], bias, ALU.add)
                    elif step == 6:
                        done = nc.vector.tensor_reduce(top["best1"][:, :], g["biased"][:, :, :], AX.X, ALU.max)
                    elif step == 7:
                        done = nc.vector.tensor_tensor(g["hit"][:, :, :], g["biased"][:, :, :], wide(top["best1"]),
                                                       ALU.is_equal)
                    elif step == 8:
                        done = nc.vector.tensor_tensor(g["rank"][:, :, :], g["hit"][:, :, :], order, ALU.mult)
                    elif step == 9:
                        done = nc.vector.tensor_reduce(top["who1"][:, :], g["rank"][:, :, :], AX.X, ALU.max)
                    elif step == 10:
                        done = nc.vector.tensor_tensor(g["first"][:, :, :], g["rank"][:, :, :], wide(top["who1"]),
                                                       ALU.is_equal)
                    elif step == 11:
                        done = nc.vector.scalar_tensor_tensor(g["rest"][:, :, :], g["first"][:, :, :], -FAR,
                                                              g["biased"][:, :, :], ALU.mult, ALU.add)
                    elif step == 12:
                        done = nc.vector.tensor_reduce(top["best2"][:, :], g["rest"][:, :, :], AX.X, ALU.max)
                    elif step == 13:
                        done = nc.vector.tensor_tensor(g["hit"][:, :, :], g["rest"][:, :, :], wide(top["best2"]),
                                                       ALU.is_equal)
                    elif step == 14:
                        done = nc.vector.tensor_tensor(g["rank"][:, :, :], g["hit"][:, :, :], order, ALU.mult)
                    elif step == 15:
                        done = nc.vector.tensor_reduce(top["who2"][:, :], g["rank"][:, :, :], AX.X, ALU.max)
                    elif step == 16:
                        done = nc.vector.tensor_tensor(g["second"][:, :, :], g["rank"][:, :, :], wide(top["who2"]),
                                                       ALU.is_equal)
                    elif step == 17:
                        done = nc.vector.tensor_tensor(g["hit"][:, :, :], g["first"][:, :, :], g["second"][:, :, :],
                                                       ALU.add)
                    elif step == 18:
                        done = nc.vector.tensor_tensor(g["gate"][:, :, :], g["hit"][:, :, :], g["score"][:, :, :],
                                                       ALU.mult)
                    elif step == 19:
                        wait_count(dve, gate_tp_done, c)
                        done = nc.vector.tensor_copy(gate_parts[:, :, 0:EXPERTS], g["gate"][:, :, :])
                    else:
                        done = nc.vector.tensor_tensor(gate_parts[:, :, EXPERTS:2 * EXPERTS], g["gate"][:, :, :],
                                                       gate_parts[:, :, 0:EXPERTS], ALU.subtract)
                    done.then_inc(gate_step, 1)

            def beside(c, e, place):
                first, last = GATE_PLACES[2 * e + place], GATE_PLACES[2 * e + place + 1]
                if not is_last(c):
                    gates(c + 1, first, last)

            def swiglu(c, slot, e):
                n, k = c * STEPS + e, (slot + e) % 2
                dve.wait_ge(silu_done, n + 1)
                dve.wait_ge(b_done, n + 1)
                wait_count(dve, hhi_done, n - 2)
                wait_count(dve, hlo_done, n - 2)
                if e == 0:
                    nc.vector.tensor_tensor(h[e % 3][:, :], silu[k][:, :], b_bank[k][:, :], ALU.mult).then_inc(prod_done, 1)
                    return
                gated = c * EXPERTS + e - 1
                wait_count(dve, h_done, gated)
                nc.vector.tensor_tensor(prod[:, :], silu[k][:, :], b_bank[k][:, :], ALU.mult).then_inc(prod_done, 1)
                beside(c, e, 0)
                dve.wait_ge(prod_done, n + 1)
                dve.wait_ge(gate_b_done, gated + 1)
                nc.vector.tensor_tensor(h[e % 3][:, :], prod[:, :], gate_bank[:, :], ALU.mult).then_inc(h_done, 1)

            def residual(c):
                dve.wait_ge(y_tok_done, c + 1)
                nc.vector.tensor_tensor(x[:, bass.ds(c * TILES, TILES), :], x[:, bass.ds(c * TILES, TILES), :],
                                        t_bank[:, :].rearrange("p (t d) -> p t d", d=P), ALU.add).then_inc(x_added, 1)

            def chunk(c, slot):
                for e in range(STEPS):
                    swiglu(c, slot, e)
                    if e == 0 and not is_last(c):
                        split_x(c + 1, 1 - slot)
                    if e == 1 and exists(c + 2):
                        norm(c + 2, slot)
                    if e == 3 and exists(c + 2):
                        scale(c + 2)
                    if e == 5 and not is_first(c):
                        residual(c - 1)
                    beside(c, e, 1)

            norm(0, 0)
            scale(0)
            split_x(0, 0)
            norm(1, 1)
            scale(1)
            gates(0, 0, GATE_STEPS)
            run_pairs(dve, chunk)
            residual(CHUNKS - 1)

        @block.tensor
        def _(pe):
            def turn_x(c):
                pe.wait_ge(ln_done, c + 1)
                wait_count(pe, x_added, c - 2)
                for t in range(TILES):
                    last = nc.tensor.transpose(t_bank[:, t * P:(t + 1) * P], xn[:, t, :], ident[:, :])
                last.then_inc(xt_done, 1)

            def router(c, slot):
                pe.wait_ge(xhi_done, c + 1)
                pe.wait_ge(xlo_done, c + 1)
                wait_count(pe, gate_t_done, c)
                for t in range(TILES):
                    tile = slice(t * P, (t + 1) * P)
                    pairs = ((xt_hi, w["router_hi"]), (xt_hi, w["router_lo"]), (xt_lo, w["router_hi"]))
                    for i, (xs, ws) in enumerate(pairs):
                        last = nc.tensor.matmul(logits[:, t, :], xs[slot][:, tile], ws[:, :],
                                                start=(i == 0), stop=(i == 2))
                last.then_inc(logits_done, 1)

            def turn_gates(c):
                pe.wait_ge(gate_step, (c + 1) * GATE_STEPS)
                for t in range(TILES):
                    last = nc.tensor.transpose(gate_tp[:, t * P:(t + 1) * P], gate_parts[:, t, :],
                                               consts["ident16"][:, :])
                last.then_inc(gate_tp_done, 1)

            def up(c, slot, e):
                n, k = c * STEPS + e, (slot + e) % 2
                if e == 0:
                    pe.wait_ge(xhi_done, c + 1)
                    pe.wait_ge(xlo_done, c + 1)
                for dst, name, free, done in ((a_bank, "w1", silu_done, a_done), (b_bank, "w3", prod_done, b_done)):
                    wait_count(pe, free, n - 1)
                    pairs = ((w[name + "_hi"], xt_hi), (w[name + "_lo"], xt_hi), (w[name + "_hi"], xt_lo))
                    for i, (ws, xs) in enumerate(pairs):
                        last = nc.tensor.matmul(dst[k][:, :], ws[:, e, :], xs[slot][:, :], start=(i == 0), stop=(i == 2))
                    last.then_inc(done, 1)

            def spread_gate(c, slot, e):
                if e == 1:
                    pe.wait_ge(gate_t_done, c + 1)
                wait_count(pe, h_done, c * EXPERTS + e - 1)
                nc.tensor.matmul(gate_bank[:, :], select_gate[:, e - 1, :], gate_t[slot][:, :],
                                 start=True, stop=True).then_inc(gate_b_done, 1)

            def down(c, slot, e):
                n, k = c * STEPS + e, e % 3
                pe.wait_ge(hhi_done, n + 1)
                pe.wait_ge(hlo_done, n + 1)
                if e == 0:
                    wait_count(pe, yt_done, c)
                pairs = ((w["w2_hi"], h_hi), (w["w2_lo"], h_hi), (w["w2_hi"], h_lo))
                for i, (ws, hs) in enumerate(pairs):
                    last = nc.tensor.matmul(y_bank[:, :], ws[:, e, :], hs[k][:, :],
                                            start=(e == 0 and i == 0), stop=(e == STEPS - 1 and i == 2))
                last.then_inc(w2_done, 1)

            def turn_y(c):
                pe.wait_ge(yt_done, c + 1)
                pe.wait_ge(xlo_done, min(c + 2, CHUNKS) if isinstance(c, int) else c + 2)
                for t in range(TILES):
                    last = nc.tensor.transpose(t_bank[:, t * P:(t + 1) * P], yt[:, t * P:(t + 1) * P], ident[:, :])
                last.then_inc(y_tok_done, 1)

            def chunk(c, slot):
                for e in range(STEPS):
                    up(c, slot, e)
                    if e == 0 and not is_last(c):
                        turn_x(c + 1)
                    if e >= LAG:
                        down(c, slot, e - LAG)
                    elif not is_first(c):
                        down(c - 1, 1 - slot, STEPS - LAG + e)
                    if e == 0:
                        turn_gates(c)
                    else:
                        spread_gate(c, slot, e)
                    if e == 1 and not is_last(c):
                        router(c + 1, 1 - slot)
                    if e == 4 and not is_first(c):
                        turn_y(c - 1)

            turn_x(0)
            router(0, 0)
            run_pairs(pe, chunk)
            for e in range(STEPS - LAG, STEPS):
                down(CHUNKS - 1, 1, e)
            turn_y(CHUNKS - 1)

        @block.scalar
        def _(act):
            def split_x(c, slot):
                act.wait_ge(xt_done, c + 1)
                wait_count(act, b_done, (c - 1) * STEPS)
                nc.scalar.activation(xt_hi[slot][:, :], t_bank[:, :], ACT.Copy).then_inc(xhi_done, 1)

            def expd(c):
                act.wait_ge(gate_step, c * GATE_STEPS + 2)
                nc.scalar.activation(g["expd"][:, :, :], g["shifted"][:, :, :], ACT.Exp).then_inc(expd_done, 1)

            def take_gates(c, slot):
                act.wait_ge(gate_tp_done, c + 1)
                wait_count(act, gate_b_done, (c - 1) * EXPERTS)
                nc.scalar.activation(gate_t[slot][:, :], gate_tp, ACT.Copy).then_inc(gate_t_done, 1)

            def silu_a(c, slot, e):
                n, k = c * STEPS + e, (slot + e) % 2
                act.wait_ge(a_done, n + 1)
                wait_count(act, prod_done, n - 1)
                nc.scalar.activation(silu[k][:, :], a_bank[k][:, :], ACT.Silu).then_inc(silu_done, 1)

            def split_h(c, slot, e):
                n, k = c * STEPS + e, e % 3
                if e == 0:
                    act.wait_ge(prod_done, n + 1)
                else:
                    act.wait_ge(h_done, c * EXPERTS + e)
                wait_count(act, w2_done, n - 2)
                wait_count(act, hlo_done, n - 2)
                nc.scalar.activation(h_hi[k][:, :], h[k][:, :], ACT.Copy).then_inc(hhi_done, 1)

            def take_y(c):
                act.wait_ge(w2_done, (c + 1) * STEPS)
                wait_count(act, y_tok_done, c)
                nc.scalar.activation(yt[:, :], y_bank[:, :], ACT.Copy, scale=0.5).then_inc(yt_done, 1)

            def chunk(c, slot):
                for e in range(STEPS):
                    if e == 3 and not is_first(c):
                        take_y(c - 1)
                    silu_a(c, slot, e)
                    if e == 0 and not is_last(c):
                        split_x(c + 1, 1 - slot)
                    if e > 0:
                        split_h(c, slot, e - 1)
                    elif not is_first(c):
                        split_h(c - 1, 1 - slot, STEPS - 1)
                    if e == 0:
                        take_gates(c, slot)
                    if e == 3 and not is_last(c):
                        expd(c + 1)

            split_x(0, 0)
            expd(0)
            run_pairs(act, chunk)
            split_h(CHUNKS - 1, 1, STEPS - 1)
            take_y(CHUNKS - 1)

        @block.gpsimd
        def _(pool):
            def low_part(c, e):
                n, k = c * STEPS + e, e % 3
                pool.wait_ge(hhi_done, n + 1)
                wait_count(pool, w2_done, n - 2)
                nc.gpsimd.tensor_tensor(h_lo[k][:, :], h[k][:, :], h_hi[k][:, :], ALU.subtract).then_inc(hlo_done, 1)

            def chunk(c, slot):
                for e in range(STEPS):
                    low_part(c, e)
                    if e == 1 and exists(c + 2):
                        norm_root(pool, nc, c + 2, buf, ln_step, ln_rooted)

            norm_root(pool, nc, 0, buf, ln_step, ln_rooted)
            norm_root(pool, nc, 1, buf, ln_step, ln_rooted)
            run_pairs(pool, chunk)




def split_weights(nc, consts, w, ffn, attn, bias, router):
    with ExitStack() as ctx:
        def sb(name, shape, dt):
            return ctx.enter_context(nc.sbuf_tensor(name, shape, dt))

        def sem(name):
            return ctx.enter_context(nc.semaphore(name))

        raw = {n: sb(f"raw_{n}", [P, STEPS, P], F32) for n in ("w1", "w3", "w2")}
        raw_router = sb("raw_router", [P, EXPERTS], F32)
        raw_attn = {n: sb(f"raw_{n}", [P, P], F32) for n in attn}
        turned_bank = ctx.enter_context(nc.psum_tensor("turned_bank", [P, 4 * P], F32))
        zeros = sb("zeros", [P, P], F32)
        loaded, zeroed, ident_done = sem("w_loaded"), sem("zeroed"), sem("ident_done")
        hi_done, lo_done, turned, tables = sem("w_hi_done"), sem("w_lo_done"), sem("w_turned"), sem("tables")
        loads = 6 + 2 + len(attn)
        names = ("w1", "w3", "w2")
        block = ctx.enter_context(nc.Block())

        @block.sync
        def _(sp):
            for n in names:
                shared, routed = ffn[n]
                sp.dma_start(raw[n][:, 0, :], shared).then_inc(loaded, DMA)
                sp.dma_start(raw[n][:, 1:STEPS, :], routed.rearrange("e d h -> d e h")).then_inc(loaded, DMA)
            sp.dma_start(raw_router[:, :], router).then_inc(loaded, DMA)
            sp.dma_start(consts["bias"][:, :], bias.rearrange("(a e) -> a e", a=1).to_broadcast([P, EXPERTS])
                         ).then_inc(loaded, DMA)
            for n in attn:
                sp.dma_start(raw_attn[n][:, :], attn[n]).then_inc(loaded, DMA)
            sp.wait_ge(loaded, loads * DMA)

        @block.gpsimd
        def _(pool):
            nc.gpsimd.memset(zeros[:, :], 0.0).then_inc(zeroed, 1)
            pool.wait_ge(zeroed, 1)
            nc.gpsimd.affine_select(out=consts["ident"][:, :], in_=zeros[:, :], compare_op=ALU.not_equal, fill=1.0,
                                    base=0, pattern=[[-1, P]], channel_multiplier=1).then_inc(ident_done, 1)
            nc.gpsimd.affine_select(out=consts["causal"][:, :], in_=zeros[:, :], compare_op=ALU.is_ge, fill=-FAR,
                                    base=0, pattern=[[-1, P]], channel_multiplier=1).then_inc(tables, 1)
            nc.gpsimd.memset(consts["eps"][:, :], LN_EPS).then_inc(tables, 1)
            nc.gpsimd.memset(consts["power"][:, :], -0.5).then_inc(tables, 1)
            for e in range(EXPERTS):
                nc.gpsimd.memset(consts["order"][:, e:e + 1], float(EXPERTS - e)).then_inc(tables, 1)

        @block.tensor
        def _(pe):
            pe.wait_ge(loaded, loads * DMA)
            pe.wait_ge(ident_done, 1)
            for i, n in enumerate(attn):
                last = nc.tensor.transpose(turned_bank[:, i * P:(i + 1) * P], raw_attn[n][:, :], consts["ident"][:, :])
            last.then_inc(turned, 1)

        @block.scalar
        def _(act):
            act.wait_ge(loaded, loads * DMA)
            for n in names:
                nc.scalar.activation(w[n + "_hi"][:, :, :], raw[n][:, :, :], ACT.Copy).then_inc(hi_done, 1)
            nc.scalar.activation(w["router_hi"][:, :], raw_router[:, :], ACT.Copy).then_inc(hi_done, 1)
            act.wait_ge(turned, 1)
            nc.scalar.activation(w["attn_hi"][:, :, :], turned_bank[:, :].rearrange("p (i n) -> p i n", n=P),
                                 ACT.Copy).then_inc(hi_done, 1)

        @block.vector
        def _(dve):
            dve.wait_ge(ident_done, 1)
            ident = consts["ident"]
            nc.vector.tensor_copy(consts["ident16"][:, :], ident[:, :]).then_inc(tables, 1)
            nc.vector.tensor_copy(consts["ident_b"][:, :], ident[:, :]).then_inc(tables, 1)
            K = 2 * EXPERTS
            nc.vector.tensor_tensor(consts["select_gate"][:, :, :],
                                    ident[0:K, 0:EXPERTS].unsqueeze(2).to_broadcast([K, EXPERTS, P]),
                                    ident[0:K, EXPERTS:K].unsqueeze(2).to_broadcast([K, EXPERTS, P]),
                                    ALU.add).then_inc(tables, 1)
            for i, n in enumerate(names):
                dve.wait_ge(hi_done, i + 1)
                nc.vector.tensor_tensor(w[n + "_lo"][:, :, :], raw[n][:, :, :], w[n + "_hi"][:, :, :],
                                        ALU.subtract).then_inc(lo_done, 1)
            dve.wait_ge(hi_done, 4)
            nc.vector.tensor_tensor(w["router_lo"][:, :], raw_router[:, :], w["router_hi"][:, :],
                                    ALU.subtract).then_inc(lo_done, 1)
            dve.wait_ge(hi_done, 5)
            nc.vector.tensor_tensor(w["attn_lo"][:, :, :], turned_bank[:, :].rearrange("p (i n) -> p i n", n=P),
                                    w["attn_hi"][:, :, :], ALU.subtract).then_inc(lo_done, 1)
            select_heads(nc, consts, tables)


def select_heads(nc, consts, tables):
    ident = consts["ident"][:, :].rearrange("p (g j d) -> p g j d", g=GROUPS, j=UNITS)
    for name, places in (("sel_q_hi", (0, 1)), ("sel_q_lo", (2,)), ("sel_k_hi", (0, 2)), ("sel_k_lo", (1,))):
        table = consts[name][:, :, :].rearrange("p g (j r) -> p g j r", r=ROWS)
        for place in range(ROWS // HEAD):
            dst = table[:, :, :, place * HEAD:(place + 1) * HEAD]
            if place in places:
                nc.vector.tensor_copy(dst, ident).then_inc(tables, 1)
            else:
                nc.vector.tensor_scalar(dst, ident, 0.0, None, ALU.mult).then_inc(tables, 1)
    nc.vector.tensor_reduce(consts["max_row"][:, :], consts["ident"][:, MAX_ROW:P:ROWS], AX.X,
                            ALU.add).then_inc(tables, 1)


PLACES = (((), ("q",), ("k",)), (("o10",), ("o11",), ("Q00",)), (("K00",), ("Q01",), ("K01",)),
          (("m10", "m11"), ("y1",), ()),
          (("z1",), ("Q10",), ("K10",)), (("o00",), ("o01",), ("Q11",)), (("K11",), ("y0",), ("v",)),
          (("m00", "m01"), ("x",), ("z0",)))
JOBS = [name for unit in PLACES for place in unit for name in place]
SHIFT = {n: -2 if n == "x" else -1 if n in ("m00", "m01") or n[0] in "qkQKv" else 1 if n in ("o10", "o11", "y1", "z1")
         else 0 for n in JOBS}


def jobs_of(turn):
    return [n for n in JOBS if exists(turn - SHIFT[n])]


def job_at(c, name):
    if isinstance(c, int):
        turn = c + SHIFT[name]
        n = sum(len(jobs_of(t)) for t in range(-2, turn)) + jobs_of(turn).index(name)
        return n % 2, n // 2
    n = sum(len(jobs_of(t)) for t in range(-2, 1)) + (SHIFT[name] - 1) * len(JOBS) + JOBS.index(name)
    return n % 2, c * (len(JOBS) // 2) + n // 2


def attention_phase(nc, x, consts, w):
    with ExitStack() as ctx:
        def sb(name, shape, dt):
            return ctx.enter_context(nc.sbuf_tensor(f"{name}_at", shape, dt))

        def bank(name):
            return ctx.enter_context(nc.psum_tensor(f"{name}_at", [P, CHUNK], F32))

        def sem(name):
            return ctx.enter_context(nc.semaphore(f"{name}_at"))

        ident, ident16 = consts["ident"], consts["ident16"]
        buf = {
            "stats": sb("stats", [P, TILES, 6], F32), "moments": sb("moments", [P, TILES, 2], F32),
            "rstd": sb("rstd", [P, TILES], F32), "var_eps": sb("var_eps", [P, TILES], F32), "power": consts["power"],
            "eps": consts["eps"], "spare": sb("spare", [P, 1], F32),
            "xn": sb("xn", [P, TILES, P], F32),
        }
        xn = buf["xn"]
        xt_hi, xt_lo = sb("xt_hi", [P, CHUNK], F16), sb("xt_lo", [P, CHUNK], F16)
        part = {n: sb(n, [P, CHUNK], F16) for n in ("q_hi", "q_lo", "k_hi", "k_lo")}
        q_pack = [sb(f"q_pack{s}", [P, GROUPS, CHUNK], F16) for s in range(2)]
        k_pack = [sb(f"k_pack{s}", [P, GROUPS, CHUNK], F16) for s in range(2)]
        v_ones = [sb(f"v_ones{s}", [P, TILES, HEADS, ROWS], F32) for s in range(2)]
        neg_max = [sb(f"neg_max{b}", [P, 2, GROUPS, UNITS, ROWS], F16) for b in range(2)]
        probs = [sb(f"probs{s}", [P, 3, CHUNK], F32) for s in range(2)]
        o_t = [sb(f"o_t{s}", [P, UNITS, SEQ], F32) for s in range(2)]
        inv = sb("inv", [P, 2, UNITS, GROUPS], F32)
        y = sb("y", [P, 2, P], F32)
        yt_hi, yt_lo = sb("yt_hi", [P, SEQ], F16), sb("yt_lo", [P, SEQ], F16)

        score_bank = [bank(f"score{s}") for s in range(2)]
        prob_bank = [bank(f"prob{i}") for i in range(3)]
        o_bank = bank("o")
        job_bank = [bank(f"job{s}") for s in range(2)]

        job_written = [sem(f"job_written{s}") for s in range(2)]
        job_taken = [sem(f"job_taken{s}") for s in range(2)]
        ln_step, ln_rooted, ln_done, buffers_set = (sem(n) for n in ("ln_step", "ln_rooted", "ln_done", "buffers_set"))
        xhi_done, qkhi_done, yhi_done, inv_done = (sem(n) for n in ("xhi_done", "qkhi_done", "yhi_done", "inv_done"))
        mask_begun = sem("mask_begun")
        scored, max_done = sem("scored"), sem("max_done")
        st_done, exp_done, masked, pv_done, o_done = (
            sem(n) for n in ("st_done", "exp_done", "masked", "pv_done", "o_done"))

        block = ctx.enter_context(nc.Block())

        def take(eng, c, name):
            k, before = job_at(c, name)
            eng.wait_ge(job_written[k], before + 1)
            return job_bank[k], job_taken[k]

        def wait_taken(eng, c, name):
            k, before = job_at(c, name)
            eng.wait_ge(job_taken[k], before + 1)

        def unit_ahead(c, slot, b, j):
            at = b * UNITS + j + UNITS + 1
            later, at = divmod(at, 2 * UNITS)
            return (c + later, (slot + later) % 2, *divmod(at, UNITS)) if exists(c + later) else None

        def packed(pack, name):
            b, half = int(name[1]), int(name[2])
            return pack[:, 2 * half:2 * half + 2, b * SEQ:(b + 1) * SEQ]

        def unit_rows(j):
            return slice(ROWS * j, ROWS * (j + 1))

        def turn_jobs(do, c, slot, names):
            for name in names:
                if exists(c - SHIFT[name]):
                    do(c - SHIFT[name], (slot - SHIFT[name]) % 2, name)

        @block.tensor
        def _(pe):
            def begin(c, name):
                k, before = job_at(c, name)
                wait_count(pe, job_taken[k], before)
                return job_bank[k], job_written[k]

            def product(dst, pairs):
                for n, (stationary, moving) in enumerate(pairs):
                    last = nc.tensor.matmul(dst, stationary, moving, start=(n == 0), stop=(n == 2))
                return last

            w_hi, w_lo = w["attn_hi"], w["attn_lo"]

            def job(c, slot, name):
                kind = name[0]
                if kind == "x":
                    pe.wait_ge(ln_done, c + 1)
                    dst, done = begin(c, name)
                    for t in range(TILES):
                        last = nc.tensor.transpose(dst[:, t * P:(t + 1) * P], xn[:, t, :], ident[:, :])
                elif kind in "qk":
                    wait_taken(pe, c, "x")
                    dst, done = begin(c, name)
                    i = "qk".index(kind)
                    last = product(dst[:, :], ((w_hi[:, i, :], xt_hi[:, :]), (w_lo[:, i, :], xt_hi[:, :]),
                                               (w_hi[:, i, :], xt_lo[:, :])))
                elif kind in "QK":
                    m, b, half = kind.lower(), int(name[1]), int(name[2])
                    wait_taken(pe, c, m)
                    dst, done = begin(c, name)
                    tokens = slice(b * SEQ, (b + 1) * SEQ)
                    for i in range(2):
                        tile = dst[:, i * SEQ:(i + 1) * SEQ]
                        nc.tensor.matmul(tile, consts[f"sel_{m}_hi"][:, 2 * half + i, :], part[m + "_hi"][:, tokens],
                                         start=True, stop=False)
                        last = nc.tensor.matmul(tile, consts[f"sel_{m}_lo"][:, 2 * half + i, :],
                                                part[m + "_lo"][:, tokens], start=False, stop=True)
                elif kind == "v":
                    dst, done = begin(c, name)
                    for t in range(TILES):
                        tile = slice(t * P, (t + 1) * P)
                        last = product(dst[:, tile], ((xt_hi[:, tile], w_hi[:, 2, :]), (xt_hi[:, tile], w_lo[:, 2, :]),
                                                      (xt_lo[:, tile], w_hi[:, 2, :])))
                elif kind == "o":
                    b, t = int(name[1]), int(name[2])
                    pe.wait_ge(o_done, c * 2 * UNITS + (b + 1) * UNITS)
                    dst, done = begin(c, name)
                    for j in range(UNITS):
                        last = nc.tensor.transpose(dst[:, j * P:(j + 1) * P], o_t[b][:, j, t * P:(t + 1) * P],
                                                   ident[:, :])
                elif kind == "y":
                    b = int(name[1])
                    wait_taken(pe, c, f"o{b}0")
                    wait_taken(pe, c, f"o{b}1")
                    dst, done = begin(c, name)
                    for t in range(2):
                        last = nc.tensor.transpose(dst[:, t * P:(t + 1) * P], y[:, t, :], ident[:, :])
                elif kind == "z":
                    wait_taken(pe, c, "y" + name[1])
                    dst, done = begin(c, name)
                    for t in range(2):
                        tile = slice(t * P, (t + 1) * P)
                        last = product(dst[:, tile], ((yt_hi[:, tile], w_hi[:, 3, :]), (yt_hi[:, tile], w_lo[:, 3, :]),
                                                      (yt_lo[:, tile], w_hi[:, 3, :])))
                elif kind == "m":
                    b, t = int(name[1]), int(name[2])
                    pe.wait_ge(max_done, c * 24 + (b + 1) * 12)
                    dst, done = begin(c, name)
                    for g in range(GROUPS):
                        last = nc.tensor.matmul(dst[:, g * P:(g + 1) * P],
                                                neg_max[b][:, t, g, :, :].rearrange("p j r -> p (j r)"), ident16[:, :],
                                                start=True, stop=True)
                last.then_inc(done, 1)

            def scores(c, slot, b, j, parts=(0, 1, 2)):
                if j == 0 and parts[0] == 0:
                    wait_taken(pe, c, f"Q{b}1")
                    wait_taken(pe, c, f"K{b}1")
                rows, first = unit_rows(j), b * SEQ
                for i in parts:
                    n = c * 24 + b * 12 + 3 * j + i
                    wait_count(pe, max_done, n - 1)
                    dst = score_bank[(3 * j + i) % 2]
                    groups = range(GROUPS) if i == 0 else range(2 * i - 2, 2 * i)
                    keys = P if i == 0 else SEQ
                    view = dst[:, :].rearrange("p (h k) -> p h k", k=keys)
                    nc.tensor.matmul(view[:, :, keys - P:keys], consts["ident_b"][:, :],
                                     consts["causal"][:, :].unsqueeze(1).to_broadcast([P, len(groups), P]),
                                     start=True, stop=False, skip_group_check=True)
                    q0 = first + (0 if i == 0 else P)
                    for h, g in enumerate(groups):
                        last = nc.tensor.matmul(view[:, h, :], q_pack[slot][rows, g, q0:q0 + P],
                                                k_pack[slot][rows, g, first:first + keys], start=False,
                                                stop=(h == len(groups) - 1), skip_group_check=True)
                    last.then_inc(scored, 1)

            def scores_t(c, slot, b, j):
                rows, first = unit_rows(j), b * SEQ
                unit = c * 2 * UNITS + b * UNITS + j
                if j == 0:
                    wait_taken(pe, c, f"m{b}0")
                    wait_taken(pe, c, f"m{b}1")
                for i in range(3):
                    wait_count(pe, exp_done, unit * 3 - 2 + i)
                    pe.wait_ge(buffers_set, 1)
                    keys = slice(first, first + P) if i < 2 else slice(first + P, first + SEQ)
                    queries = slice(keys.start, first + SEQ)
                    width = queries.stop - queries.start
                    for h, g in enumerate(range(2 * i, 2 * i + 2) if i < 2 else range(GROUPS)):
                        last = nc.tensor.matmul(prob_bank[i][:, h * width:(h + 1) * width],
                                                k_pack[slot][rows, g, keys], q_pack[slot][rows, g, queries],
                                                start=True, stop=True)
                    last.then_inc(st_done, 1)

            def weigh(c, slot, b, j):
                unit = c * 2 * UNITS + b * UNITS + j
                if j == 0 and b == 0:
                    wait_taken(pe, c, "v")
                pe.wait_ge(masked, unit * 2 + 2)
                wait_count(pe, o_done, unit)
                for t in range(2):
                    for g in range(GROUPS):
                        src = (probs[j % 2][:, g // 2, (g % 2) * SEQ:(g % 2 + 1) * SEQ] if t == 0
                               else probs[j % 2][:, 2, g * P:(g + 1) * P])
                        last = nc.tensor.matmul(o_bank[g * ROWS:(g + 1) * ROWS, t * P:SEQ],
                                                v_ones[slot][:, 2 * b + t, GROUPS * g + j, :], src,
                                                start=(t == 0), stop=(t == 1), skip_group_check=True)
                last.then_inc(pv_done, 1)

            def turn(c, slot):
                for b in range(2):
                    for j in range(UNITS):
                        scores_t(c, slot, b, j)
                        places = PLACES[b * UNITS + j]
                        turn_jobs(job, c, slot, places[0])
                        ahead = unit_ahead(c, slot, b, j)
                        if ahead:
                            scores(*ahead, parts=(0, 1))
                        turn_jobs(job, c, slot, places[1])
                        if j > 0:
                            weigh(c, slot, b, j - 1)
                        elif b == 1:
                            weigh(c, slot, 0, UNITS - 1)
                        elif exists(c - 1):
                            weigh(c - 1, 1 - slot, 1, UNITS - 1)
                        if ahead:
                            scores(*ahead, parts=(2,))
                        turn_jobs(job, c, slot, places[2])

            turn_jobs(job, -2, 0, ("x",))
            turn_jobs(job, -1, 1, JOBS[:-4])
            for j in range(UNITS):
                scores(0, 0, 0, j)
            turn_jobs(job, -1, 1, JOBS[-4:])
            scores(0, 0, 1, 0)
            run_pairs(pe, turn)
            weigh(CHUNKS - 1, 1, 1, UNITS - 1)
            turn_jobs(job, CHUNKS, 0, JOBS)

        @block.vector
        def _(dve):
            def norm(c):
                norm_stats(dve, nc, c, x, buf, ln_step, ln_done)

            def scale(c):
                if not is_first(c):
                    wait_taken(dve, c - 1, "x")
                norm_scale(dve, nc, c, x, buf, ln_rooted, ln_done)

            def job(c, slot, name):
                kind = name[0]
                if kind in "Kv":
                    return
                src, done = take(dve, c, name)
                if kind == "x":
                    dve.wait_ge(xhi_done, c + 1)
                    last = nc.vector.tensor_tensor(xt_lo[:, :], src[:, :], xt_hi[:, :], ALU.subtract)
                elif kind in "qk":
                    dve.wait_ge(qkhi_done, c * 2 + (1 if kind == "q" else 2))
                    last = nc.vector.tensor_tensor(part[kind + "_lo"][:, :], src[:, :], part[kind + "_hi"][:, :],
                                                   ALU.subtract)
                elif kind == "Q":
                    wait_count(dve, st_done, (c - 1) * 6 * UNITS)
                    last = nc.vector.tensor_copy(packed(q_pack[slot], name),
                                                 src[:, :].rearrange("p (g n) -> p g n", n=SEQ))
                elif kind == "m":
                    first = int(name[1]) * SEQ + int(name[2]) * P
                    q = q_pack[slot][:, :, first:first + P]
                    last = nc.vector.tensor_tensor(q, src[:, :].rearrange("p (g q) -> p g q", q=P), q, ALU.add)
                elif kind == "o":
                    b, t = int(name[1]), int(name[2])
                    o = src[:, :].rearrange("p (j g r) -> p j g r", j=UNITS, r=ROWS)
                    nc.vector.reciprocal(inv[:, t, :, :], o[:, :, :, HEAD]).then_inc(inv_done, 1)
                    dve.wait_ge(inv_done, c * 4 + 2 * b + t + 1)
                    last = nc.vector.tensor_tensor(y[:, t, :].rearrange("p (g j d) -> p j g d", j=UNITS, d=HEAD),
                                                   o[:, :, :, 0:HEAD],
                                                   inv[:, t, :, :].unsqueeze(3).to_broadcast([P, UNITS, GROUPS, HEAD]),
                                                   ALU.mult)
                elif kind == "y":
                    dve.wait_ge(yhi_done, c * 2 + int(name[1]) + 1)
                    last = nc.vector.tensor_tensor(yt_lo[:, :], src[:, 0:SEQ], yt_hi[:, :], ALU.subtract)
                elif kind == "z":
                    rows = x[:, bass.ds(c * TILES + 2 * int(name[1]), 2), :]
                    last = nc.vector.tensor_tensor(rows, rows, src[:, 0:SEQ].rearrange("p (t d) -> p t d", d=P),
                                                   ALU.add)
                last.then_inc(done, 1)

            def maxima(c, b, j, parts=(0, 1, 2)):
                for i in parts:
                    n = c * 24 + b * 12 + 3 * j + i
                    dve.wait_ge(scored, n + 1)
                    src = score_bank[(3 * j + i) % 2][:, :].rearrange("p (h k) -> p h k", k=P if i == 0 else SEQ)
                    dst = (neg_max[b][:, 0, :, j, MAX_ROW] if i == 0 else neg_max[b][:, 1, 2 * i - 2:2 * i, j, MAX_ROW])
                    nc.vector.tensor_reduce(dst, src, AX.X, ALU.max, negate=True).then_inc(max_done, 1)

            def turn(c, slot):
                for b in range(2):
                    for j in range(UNITS):
                        places = PLACES[b * UNITS + j]
                        turn_jobs(job, c, slot, places[0])
                        ahead = unit_ahead(c, slot, b, j)
                        if ahead:
                            maxima(ahead[0], *ahead[2:], parts=(0, 1))
                        turn_jobs(job, c, slot, places[1])
                        if ahead:
                            maxima(ahead[0], *ahead[2:], parts=(2,))
                        if b == 1 and j == 1 and exists(c + 2):
                            norm(c + 2)
                        if b == 1 and j == 2 and exists(c + 2):
                            scale(c + 2)
                        turn_jobs(job, c, slot, places[2])

            for s in range(2):
                nc.vector.memset(neg_max[s][:, :, :, :, :].rearrange("p a b c d -> p (a b c d)"), 0.0)
                v = v_ones[s][:, :, :, :].rearrange("p t h r -> p (t h) r")
                nc.vector.memset(v[:, :, HEAD + 1:ROWS], 0.0)
                last = nc.vector.memset(v[:, :, HEAD:HEAD + 1], 1.0)
            last.then_inc(buffers_set, 1)
            norm(0)
            scale(0)
            turn_jobs(job, -2, 0, ("x",))
            turn_jobs(job, -1, 1, JOBS[:-4])
            norm(1)
            scale(1)
            dve.wait_ge(buffers_set, 1)
            for j in range(UNITS):
                maxima(0, 0, j)
            turn_jobs(job, -1, 1, JOBS[-4:])
            maxima(0, 1, 0)
            run_pairs(dve, turn)
            turn_jobs(job, CHUNKS, 0, JOBS)

        @block.scalar
        def _(act):
            def job(c, slot, name):
                kind = name[0]
                if kind in "Qmoz":
                    return
                if kind == "y":
                    b = int(name[1])
                    if b == 1:
                        wait_taken(act, c, "z0")
                    elif not is_first(c):
                        wait_taken(act, c - 1, "z1")
                src, done = take(act, c, name)
                if kind == "x":
                    nc.scalar.activation(xt_hi[:, :], src[:, :], ACT.Copy).then_inc(xhi_done, 1)
                elif kind in "qk":
                    nc.scalar.activation(part[kind + "_hi"][:, :], src[:, :], ACT.Copy).then_inc(qkhi_done, 1)
                elif kind == "K":
                    nc.scalar.activation(packed(k_pack[slot], name), src[:, :].rearrange("p (g n) -> p g n", n=SEQ),
                                         ACT.Identity, bias=consts["max_row"][:, :]).then_inc(done, 1)
                elif kind == "v":
                    nc.scalar.activation(v_ones[slot][:, :, :, 0:HEAD],
                                         src[:, :].rearrange("p (t h d) -> p t h d", t=TILES, d=HEAD),
                                         ACT.Copy).then_inc(done, 1)
                elif kind == "y":
                    nc.scalar.activation(yt_hi[:, :], src[:, 0:SEQ], ACT.Copy).then_inc(yhi_done, 1)

            def exponents(c, b, j):
                unit = c * 2 * UNITS + b * UNITS + j
                for i in range(3):
                    act.wait_ge(st_done, unit * 3 + i + 1)
                    if i == 0:
                        wait_count(act, pv_done, unit - 1)
                    nc.scalar.activation(probs[j % 2][:, i, :], prob_bank[i][:, :], ACT.Exp,
                                         scale=SCALE).then_inc(exp_done, 1)

            def take_o(c, b, j):
                unit = c * 2 * UNITS + b * UNITS + j
                act.wait_ge(pv_done, unit + 1)
                nc.scalar.activation(o_t[b][:, j, :], o_bank[:, 0:SEQ], ACT.Copy).then_inc(o_done, 1)

            def turn(c, slot):
                for b in range(2):
                    for j in range(UNITS):
                        exponents(c, b, j)
                        places = PLACES[b * UNITS + j]
                        turn_jobs(job, c, slot, places[0])
                        turn_jobs(job, c, slot, places[1])
                        if j > 0:
                            take_o(c, b, j - 1)
                        elif b == 1:
                            take_o(c, 0, UNITS - 1)
                        elif exists(c - 1):
                            take_o(c - 1, 1, UNITS - 1)
                        turn_jobs(job, c, slot, places[2])

            act.wait_ge(buffers_set, 1)
            turn_jobs(job, -2, 0, ("x",))
            turn_jobs(job, -1, 1, JOBS)
            run_pairs(act, turn)
            take_o(CHUNKS - 1, 1, UNITS - 1)
            turn_jobs(job, CHUNKS, 0, JOBS)

        @block.gpsimd
        def _(pool):
            def mask(c, b, j):
                unit = c * 2 * UNITS + b * UNITS + j
                for i in range(2):
                    pool.wait_ge(exp_done, unit * 3 + 2 + i)
                    pool.sem_inc(mask_begun, 1)
                    p = (probs[j % 2][:, 0:2, :].rearrange("p i (h q) -> p (i h) q", q=SEQ)[:, :, 0:P] if i == 0
                         else probs[j % 2][:, 2, :].rearrange("p (h q) -> p h q", q=P))
                    nc.gpsimd.affine_select(out=p, in_=p, compare_op=ALU.is_ge, fill=0.0, base=0,
                                            pattern=[[0, GROUPS], [1, P]], channel_multiplier=-1).then_inc(masked, 1)

            def turn(c, slot):
                for b in range(2):
                    for j in range(UNITS):
                        mask(c, b, j)
                        if b == 1 and j == 1 and exists(c + 2):
                            norm_root(pool, nc, c + 2, buf, ln_step, ln_rooted)

            norm_root(pool, nc, 0, buf, ln_step, ln_rooted)
            norm_root(pool, nc, 1, buf, ln_step, ln_rooted)
            run_pairs(pool, turn)



def macaron_kernel(nc, L0_attn_x, L0_attn_W_Q, L0_attn_W_K, L0_attn_W_V, L0_attn_W_O, L0_ffn_router_w,
                   L0_ffn_expert_bias, L0_ffn_w1, L0_ffn_w2, L0_ffn_w3, L0_ffn_sw1, L0_ffn_sw2, L0_ffn_sw3, out):
    with ExitStack() as ctx:
        def sb(name, shape, dt):
            return ctx.enter_context(nc.sbuf_tensor(name, shape, dt))

        x = sb("x", [P, CHUNKS * TILES, P], F32)
        consts = {
            "ident": sb("ident", [P, P], F32), "ident16": sb("ident16", [P, P], F16),
            "ident_b": sb("ident_b", [P, P], BF16), "causal": sb("causal", [P, P], BF16),
            "bias": sb("bias", [P, EXPERTS], F32), "order": sb("order", [P, EXPERTS], F32),
            "power": sb("power", [P, TILES], F32), "eps": sb("eps", [P, TILES], F32),
            "max_row": sb("max_row", [P, 1], F32),
            "select_gate": sb("select_gate", [2 * EXPERTS, EXPERTS, P], F16),
        }
        for n in ("sel_q_hi", "sel_q_lo", "sel_k_hi", "sel_k_lo"):
            consts[n] = sb(n, [P, GROUPS, P], F16)
        w = {f"{n}_{part}": sb(f"{n}_{part}", [P, STEPS, P], F16)
             for n in ("w1", "w3", "w2") for part in ("hi", "lo")}
        for part in ("hi", "lo"):
            w["router_" + part] = sb("router_" + part, [P, EXPERTS], F16)
            w["attn_" + part] = sb("attn_" + part, [P, 4, P], F16)
        ffn = {"w1": (L0_ffn_sw1, L0_ffn_w1), "w3": (L0_ffn_sw3, L0_ffn_w3), "w2": (L0_ffn_sw2, L0_ffn_w2)}
        attn = {"wq": L0_attn_W_Q, "wk": L0_attn_W_K, "wv": L0_attn_W_V, "wo": L0_attn_W_O}
        x_dram = L0_attn_x.rearrange("b s d -> (b s) d")
        out_dram = out.rearrange("b s d -> (b s) d")

        split_weights(nc, consts, w, ffn, attn, L0_ffn_expert_bias, L0_ffn_router_w)
        ffn_phase(nc, x, consts, w, 0, x_dram, None)
        attention_phase(nc, x, consts, w)
        ffn_phase(nc, x, consts, w, 1, None, out_dram)


_INS = ['L0_attn_x', 'L0_attn_W_Q', 'L0_attn_W_K', 'L0_attn_W_V', 'L0_attn_W_O', 'L0_ffn_router_w',
        'L0_ffn_expert_bias', 'L0_ffn_w1', 'L0_ffn_w2', 'L0_ffn_w3', 'L0_ffn_sw1', 'L0_ffn_sw2', 'L0_ffn_sw3']
_OUTS = [((32, 256, 128), 'float32')]


def kernel(**inputs):
    import numpy as _np
    import concourse.bacc as _bacc
    from concourse import mybir as _mybir
    from concourse.bass_utils import run_bass_kernel_spmd as _run

    nc = _bacc.Bacc("TRN2", target_bir_lowering=False, num_devices=1)
    arrays, args = {}, []
    for name in _INS:
        a = _np.ascontiguousarray(inputs[name])
        arrays[f"in_{name}_dram"] = a
        args.append(nc.dram_tensor(f"in_{name}_dram", a.shape, _mybir.dt.from_np(a.dtype), kind="ExternalInput").ap())
    for i, (shape, dtype) in enumerate(_OUTS):
        dt = _mybir.dt.from_np(_np.dtype(dtype))
        args.append(nc.dram_tensor(f"out_{i}_dram", shape, dt, kind="ExternalOutput").ap())
    macaron_kernel(nc, *args)
    r = _run(nc, [arrays], core_ids=[0])
    got = tuple(r.results[0][f"out_{i}_dram"] for i in range(len(_OUTS)))
    return got[0]
```

```python
from contextlib import ExitStack

import concourse.bass as bass
from concourse import mybir

ALU = mybir.AluOpType
ACT = mybir.ActivationFunctionType
AX = mybir.AxisListType
F32 = mybir.dt.float32
F16 = mybir.dt.float16
BF16 = mybir.dt.bfloat16

P = 128
SEQ = 256
TILES = 4
CHUNK = TILES * P
CHUNKS = 32 * SEQ // CHUNK
EXPERTS = 8
STEPS = EXPERTS + 1
LAG = 3
LN_EPS = 1e-5
HEADS = 16
HEAD = P // HEADS
GROUPS = 4
ROWS = P // GROUPS
MAX_ROW = 3 * HEAD
SCALE = float(HEAD) ** -0.5
UNITS = 4
FAR = 1e30
GATE_PLACES = (0, 0, 0, 0, 0, 0, 0, 2, 2, 4, 5, 7, 7, 9, 10, 12, 13, 15, 16)
GATE_STEPS = 21
DMA = 16


def run_pairs(eng, chunk):
    chunk(0, 0)
    chunk(1, 1)
    with eng.Fori(1, CHUNKS // 2 - 1) as pair:
        chunk(pair * 2, 0)
        chunk(pair * 2 + 1, 1)
    chunk(CHUNKS - 2, 0)
    chunk(CHUNKS - 1, 1)


def is_first(c):
    return isinstance(c, int) and c == 0


def is_last(c):
    return isinstance(c, int) and c == CHUNKS - 1


def exists(c):
    return not isinstance(c, int) or 0 <= c < CHUNKS


def wait_count(eng, sem, value):
    if not isinstance(value, int) or value > 0:
        eng.wait_ge(sem, value)


LN_STEPS = 2 * TILES


def chunk_rows(x, c):
    first = (c - CHUNKS if isinstance(c, int) and c >= CHUNKS else c) * TILES
    return lambda t: x[:, first + t, :]


def norm_stats(dve, nc, c, rows, buf, step, scaled):
    base = c * LN_STEPS
    wait_count(dve, scaled, c)
    for t in range(TILES):
        nc.vector.bn_stats(buf["stats"][:, t, :], rows(t)).then_inc(step, 1)
    dve.wait_ge(step, base + TILES)
    nc.vector.memset(buf["spare"][:, :], 0.0)
    for t in range(TILES):
        nc.vector.bn_aggr(buf["moments"][:, t, :], buf["stats"][:, t, :]).then_inc(step, 1)


def norm_root(pool, nc, c, buf, step, rooted):
    pool.wait_ge(step, (c + 1) * LN_STEPS)
    nc.gpsimd.tensor_tensor(buf["var_eps"][:, :], buf["moments"][:, :, 1], buf["eps"][:, :], ALU.add).then_inc(rooted, 1)
    pool.wait_ge(rooted, 2 * c + 1)
    nc.gpsimd.tensor_tensor(buf["rstd"][:, :], buf["var_eps"][:, :], buf["power"][:, :], ALU.pow).then_inc(rooted, 1)


def norm_scale(dve, nc, c, rows, buf, rooted, scaled):
    dve.wait_ge(rooted, 2 * c + 2)
    for t in range(TILES):
        last = nc.vector.tensor_scalar(buf["xn"][:, t, :], rows(t), buf["moments"][:, t, 0:1],
                                       buf["rstd"][:, t:t + 1], ALU.subtract, ALU.mult)
    last.then_inc(scaled, 1)


WEIGHTS = ("w1", "w3", "w2", "router", "attn")


class WeightPreparation:

    def __init__(self, nc, ctx, consts, w, ffn, attn, bias, router):
        def sb(name, shape, dt):
            return ctx.enter_context(nc.sbuf_tensor(name, shape, dt))

        def sem(name):
            return ctx.enter_context(nc.semaphore(name))

        self.nc, self.consts, self.w = nc, consts, w
        self.ffn, self.attn, self.bias, self.router = ffn, attn, bias, router
        self.raw = {n: sb(f"raw_{n}", [P, STEPS, P], F32) for n in ("w1", "w3", "w2")}
        self.raw["router"] = sb("raw_router", [P, EXPERTS], F32)
        self.raw["attn"] = sb("raw_attn", [P, len(attn), P], F32)
        self.zeros = sb("zeros", [P, P], F32)
        self.loaded = {n: sem(f"{n}_loaded") for n in WEIGHTS}
        self.hi_done = {n: sem(f"{n}_hi_done") for n in WEIGHTS}
        self.lo_done = {n: sem(f"{n}_lo_done") for n in WEIGHTS}
        self.bias_loaded, self.zeroed, self.ident_done = sem("bias_loaded"), sem("zeroed"), sem("ident_done")
        self.pool_tables, self.dve_tables, self.attn_turned = sem("pool_tables"), sem("dve_tables"), sem("attn_turned")

    def view(self, name):
        return self.raw[name][:, :] if name == "router" else self.raw[name][:, :, :]

    def part(self, name, which):
        t = self.w[f"{name}_{which}"]
        return t[:, :] if name == "router" else t[:, :, :]

    def load(self, sp):
        for n in ("w1", "w3", "w2"):
            shared, routed = self.ffn[n]
            sp.dma_start(self.raw[n][:, 0, :], shared).then_inc(self.loaded[n], DMA)
            sp.dma_start(self.raw[n][:, 1:STEPS, :], routed.rearrange("e d h -> d e h")).then_inc(self.loaded[n], DMA)
            if n == "w1":
                sp.dma_start(self.raw["router"][:, :], self.router).then_inc(self.loaded["router"], DMA)
                sp.dma_start(self.consts["bias"][:, :],
                             self.bias.rearrange("(a e) -> a e", a=1).to_broadcast([P, EXPERTS])
                             ).then_inc(self.bias_loaded, DMA)
        for i, n in enumerate(self.attn):
            sp.dma_start(self.raw["attn"][:, i, :], self.attn[n]).then_inc(self.loaded["attn"], DMA)

    def loads(self, name):
        return {"router": 1, "attn": len(self.attn)}.get(name, 2) * DMA

    def pool_consts(self, pool):
        nc, consts = self.nc, self.consts
        nc.gpsimd.memset(self.zeros[:, :], 0.0).then_inc(self.zeroed, 1)
        pool.wait_ge(self.zeroed, 1)
        nc.gpsimd.affine_select(out=consts["ident"][:, :], in_=self.zeros[:, :], compare_op=ALU.not_equal, fill=1.0,
                                base=0, pattern=[[-1, P]], channel_multiplier=1).then_inc(self.ident_done, 1)
        nc.gpsimd.affine_select(out=consts["causal"][:, :], in_=self.zeros[:, :], compare_op=ALU.is_ge, fill=-FAR,
                                base=0, pattern=[[-1, P]], channel_multiplier=1).then_inc(self.pool_tables, 1)
        nc.gpsimd.memset(consts["eps"][:, :], LN_EPS).then_inc(self.pool_tables, 1)
        nc.gpsimd.memset(consts["power"][:, :], -0.5).then_inc(self.pool_tables, 1)
        for e in range(EXPERTS):
            nc.gpsimd.memset(consts["order"][:, e:e + 1], float(EXPERTS - e)).then_inc(self.pool_tables, 1)

    def wait_pool_tables(self, eng):
        eng.wait_ge(self.pool_tables, 3 + EXPERTS)

    def dve_consts(self, dve):
        nc, consts = self.nc, self.consts
        dve.wait_ge(self.ident_done, 1)
        ident = consts["ident"]
        nc.vector.tensor_copy(consts["ident16"][:, :], ident[:, :]).then_inc(self.dve_tables, 1)
        nc.vector.tensor_copy(consts["ident_b"][:, :], ident[:, :]).then_inc(self.dve_tables, 1)
        K = 2 * EXPERTS
        nc.vector.tensor_tensor(consts["select_gate"][:, :, :],
                                ident[0:K, 0:EXPERTS].unsqueeze(2).to_broadcast([K, EXPERTS, P]),
                                ident[0:K, EXPERTS:K].unsqueeze(2).to_broadcast([K, EXPERTS, P]),
                                ALU.add).then_inc(self.dve_tables, 1)

    def wait_dve_tables(self, eng):
        eng.wait_ge(self.dve_tables, 3)

    def turn_attn(self, pe, bank):
        pe.wait_ge(self.loaded["attn"], self.loads("attn"))
        for i in range(len(self.attn)):
            last = self.nc.tensor.transpose(bank[:, i * P:(i + 1) * P], self.raw["attn"][:, i, :],
                                            self.consts["ident"][:, :])
        last.then_inc(self.attn_turned, 1)

    def high(self, act, name, bank=None):
        if name == "attn":
            act.wait_ge(self.attn_turned, 1)
            src = bank[:, :].rearrange("p (i n) -> p i n", n=P)
        else:
            act.wait_ge(self.loaded[name], self.loads(name))
            src = self.view(name)
        self.nc.scalar.activation(self.part(name, "hi"), src, ACT.Copy).then_inc(self.hi_done[name], 1)

    def low(self, eng, engine, name, bank=None):
        eng.wait_ge(self.hi_done[name], 1)
        src = bank[:, :].rearrange("p (i n) -> p i n", n=P) if name == "attn" else self.view(name)
        engine.tensor_tensor(self.part(name, "lo"), src, self.part(name, "hi"),
                             ALU.subtract).then_inc(self.lo_done[name], 1)

    def wait_split(self, eng, name):
        eng.wait_ge(self.lo_done[name], 1)


def ffn_phase(nc, x, consts, w, norms, phase, x_dram, out, prepare=None):
    with ExitStack() as ctx:
        def sb(name, shape, dt):
            return ctx.enter_context(nc.sbuf_tensor(f"{name}_{phase}", shape, dt))

        def bank(name):
            return ctx.enter_context(nc.psum_tensor(f"{name}_{phase}", [P, CHUNK], F32))

        def sem(name):
            return ctx.enter_context(nc.semaphore(f"{name}_{phase}"))

        ident, select_gate = consts["ident"], consts["select_gate"]
        buf, xn = norms, norms["xn"]
        ln_step, ln_rooted, ln_done = norms["step"], norms["rooted"], norms["done"]
        xt_hi, xt_lo = norms["xt_hi"], norms["xt_lo"]
        norm0 = 2 * CHUNKS * phase
        made = 1 if phase > 0 else 0
        more = 1 if out is None else 0
        silu = [sb(f"silu{s}", [P, CHUNK], F32) for s in range(2)]
        prod = sb("prod", [P, CHUNK], F32)
        h = [sb(f"h{s}", [P, CHUNK], F32) for s in range(3)]
        h_hi = [sb(f"h_hi{s}", [P, CHUNK], F16) for s in range(3)]
        h_lo = [sb(f"h_lo{s}", [P, CHUNK], F16) for s in range(3)]
        yt = sb("yt", [P, CHUNK], F32)
        gate_t = [sb(f"gate_t{s}", [2 * EXPERTS, CHUNK], F16) for s in range(2)]
        g = {n: sb(n, [P, TILES, EXPERTS], F32) for n in
             ("shifted", "expd", "score", "biased", "hit", "rank", "first", "rest", "second", "gate")}
        top = {n: sb(n, [P, TILES], F32) for n in ("peak", "total", "inverse", "best1", "who1", "best2", "who2")}
        gate_parts = sb("gate_parts", [P, TILES, 2 * EXPERTS], F16)

        a_bank = [bank(f"a{s}") for s in range(2)]
        b_bank = [bank(f"b{s}") for s in range(2)]
        gate_bank, y_bank, t_bank, r_bank = bank("gate_b"), bank("y_b"), bank("t_b"), bank("r_b")
        logits = r_bank[:, 0:TILES * EXPERTS].rearrange("p (t e) -> p t e", e=EXPERTS)
        gate_tp = r_bank[0:2 * EXPERTS, 256:512].bitcast(F16)

        x_loaded = [sem(f"x_loaded{s}") for s in range(2)]
        xt_done, xhi_done, xlo_done = (sem(n) for n in ("xt_done", "xhi_done", "xlo_done"))
        logits_done, gate_step, expd_done, gate_tp_done, gate_t_done = (
            sem(n) for n in ("logits_done", "gate_step", "expd_done", "gate_tp_done", "gate_t_done"))
        a_done, b_done, silu_done, prod_done, gate_b_done, h_done = (
            sem(n) for n in ("a_done", "b_done", "silu_done", "prod_done", "gate_b_done", "h_done"))
        hhi_done, hlo_done, w2_done, yt_done, y_tok_done, x_added, stored = (
            sem(n) for n in ("hhi_done", "hlo_done", "w2_done", "yt_done", "y_tok_done", "x_added", "stored"))

        block = ctx.enter_context(nc.Block())

        @block.sync
        def _(sp):
            if x_dram is not None:
                src = x_dram.rearrange("(c p) d -> p c d", p=P)
                for c in range(CHUNKS):
                    if c == 1:
                        prepare.load(sp)
                    wait_count(sp, x_loaded[c % 2], c // 2 * DMA)
                    sp.dma_start(x[:, c * TILES:(c + 1) * TILES, :],
                                 src[:, c * TILES:(c + 1) * TILES, :]).then_inc(x_loaded[c % 2], DMA)
            if out is not None:
                dst = out.rearrange("(c p) d -> p c d", p=P)
                with sp.Fori(0, CHUNKS) as c:
                    sp.wait_ge(x_added, c + 1)
                    sp.dma_start(dst[:, bass.ds(c * TILES, TILES), :],
                                 x[:, bass.ds(c * TILES, TILES), :]).then_inc(stored, DMA)
                sp.wait_ge(stored, CHUNKS * DMA)

        @block.vector
        def _(dve):
            def norm(c, slot):
                if isinstance(c, int) and c >= CHUNKS:
                    dve.wait_ge(x_added, c - CHUNKS + 1)
                elif x_dram is not None:
                    dve.wait_ge(x_loaded[slot], ((c - slot) // 2 + 1) * DMA if isinstance(c, int)
                                else (c - slot) * (DMA // 2) + DMA)
                norm_stats(dve, nc, norm0 + c, chunk_rows(x, c), buf, ln_step, ln_done)

            def scale(c):
                wait_count(dve, xt_done, c - made)
                norm_scale(dve, nc, norm0 + c, chunk_rows(x, c), buf, ln_rooted, ln_done)

            def split_x(c, slot):
                dve.wait_ge(xhi_done, c + 1 - made)
                nc.vector.tensor_tensor(xt_lo[slot][:, :], t_bank[:, :], xt_hi[slot][:, :],
                                        ALU.subtract).then_inc(xlo_done, 1)

            def gates(c, first, last):
                def wide(v):
                    return v[:, :].unsqueeze(2).to_broadcast([P, TILES, EXPERTS])

                bias = consts["bias"][:, :].unsqueeze(1).to_broadcast([P, TILES, EXPERTS])
                order = consts["order"][:, :].unsqueeze(1).to_broadcast([P, TILES, EXPERTS])
                for step in range(first, last):
                    if step == 0:
                        dve.wait_ge(logits_done, c + 1)
                    elif step == 2:
                        dve.wait_ge(expd_done, c + 1)
                    else:
                        dve.wait_ge(gate_step, c * GATE_STEPS + step)
                    if step == 0:
                        done = nc.vector.tensor_reduce(top["peak"][:, :], logits, AX.X, ALU.max)
                    elif step == 1:
                        done = nc.vector.tensor_tensor(g["shifted"][:, :, :], logits, wide(top["peak"]), ALU.subtract)
                    elif step == 2:
                        done = nc.vector.tensor_reduce(top["total"][:, :], g["expd"][:, :, :], AX.X, ALU.add)
                    elif step == 3:
                        done = nc.vector.reciprocal(top["inverse"][:, :], top["total"][:, :])
                    elif step == 4:
                        done = nc.vector.tensor_tensor(g["score"][:, :, :], g["expd"][:, :, :], wide(top["inverse"]),
                                                       ALU.mult)
                    elif step == 5:
                        done = nc.vector.tensor_tensor(g["biased"][:, :, :], g["score"][:, :, :], bias, ALU.add)
                    elif step == 6:
                        done = nc.vector.tensor_reduce(top["best1"][:, :], g["biased"][:, :, :], AX.X, ALU.max)
                    elif step == 7:
                        done = nc.vector.tensor_tensor(g["hit"][:, :, :], g["biased"][:, :, :], wide(top["best1"]),
                                                       ALU.is_equal)
                    elif step == 8:
                        done = nc.vector.tensor_tensor(g["rank"][:, :, :], g["hit"][:, :, :], order, ALU.mult)
                    elif step == 9:
                        done = nc.vector.tensor_reduce(top["who1"][:, :], g["rank"][:, :, :], AX.X, ALU.max)
                    elif step == 10:
                        done = nc.vector.tensor_tensor(g["first"][:, :, :], g["rank"][:, :, :], wide(top["who1"]),
                                                       ALU.is_equal)
                    elif step == 11:
                        done = nc.vector.scalar_tensor_tensor(g["rest"][:, :, :], g["first"][:, :, :], -FAR,
                                                              g["biased"][:, :, :], ALU.mult, ALU.add)
                    elif step == 12:
                        done = nc.vector.tensor_reduce(top["best2"][:, :], g["rest"][:, :, :], AX.X, ALU.max)
                    elif step == 13:
                        done = nc.vector.tensor_tensor(g["hit"][:, :, :], g["rest"][:, :, :], wide(top["best2"]),
                                                       ALU.is_equal)
                    elif step == 14:
                        done = nc.vector.tensor_tensor(g["rank"][:, :, :], g["hit"][:, :, :], order, ALU.mult)
                    elif step == 15:
                        done = nc.vector.tensor_reduce(top["who2"][:, :], g["rank"][:, :, :], AX.X, ALU.max)
                    elif step == 16:
                        done = nc.vector.tensor_tensor(g["second"][:, :, :], g["rank"][:, :, :], wide(top["who2"]),
                                                       ALU.is_equal)
                    elif step == 17:
                        done = nc.vector.tensor_tensor(g["hit"][:, :, :], g["first"][:, :, :], g["second"][:, :, :],
                                                       ALU.add)
                    elif step == 18:
                        done = nc.vector.tensor_tensor(g["gate"][:, :, :], g["hit"][:, :, :], g["score"][:, :, :],
                                                       ALU.mult)
                    elif step == 19:
                        wait_count(dve, gate_tp_done, c)
                        done = nc.vector.tensor_copy(gate_parts[:, :, 0:EXPERTS], g["gate"][:, :, :])
                    else:
                        done = nc.vector.tensor_tensor(gate_parts[:, :, EXPERTS:2 * EXPERTS], g["gate"][:, :, :],
                                                       gate_parts[:, :, 0:EXPERTS], ALU.subtract)
                    done.then_inc(gate_step, 1)

            def beside(c, e, place):
                first, last = GATE_PLACES[2 * e + place], GATE_PLACES[2 * e + place + 1]
                if not is_last(c):
                    gates(c + 1, first, last)

            def swiglu(c, slot, e):
                n, k = c * STEPS + e, (slot + e) % 2
                dve.wait_ge(silu_done, n + 1)
                dve.wait_ge(b_done, n + 1)
                wait_count(dve, hhi_done, n - 2)
                wait_count(dve, hlo_done, n - 2)
                if e == 0:
                    nc.vector.tensor_tensor(h[e % 3][:, :], silu[k][:, :], b_bank[k][:, :], ALU.mult).then_inc(prod_done, 1)
                    return
                gated = c * EXPERTS + e - 1
                wait_count(dve, h_done, gated)
                nc.vector.tensor_tensor(prod[:, :], silu[k][:, :], b_bank[k][:, :], ALU.mult).then_inc(prod_done, 1)
                beside(c, e, 0)
                dve.wait_ge(prod_done, n + 1)
                dve.wait_ge(gate_b_done, gated + 1)
                nc.vector.tensor_tensor(h[e % 3][:, :], prod[:, :], gate_bank[:, :], ALU.mult).then_inc(h_done, 1)

            def residual(c):
                dve.wait_ge(y_tok_done, c + 1)
                nc.vector.tensor_tensor(x[:, bass.ds(c * TILES, TILES), :], x[:, bass.ds(c * TILES, TILES), :],
                                        t_bank[:, :].rearrange("p (t d) -> p t d", d=P), ALU.add).then_inc(x_added, 1)

            def chunk(c, slot):
                for e in range(STEPS):
                    swiglu(c, slot, e)
                    if e == 0 and exists(c + 1 - more):
                        split_x(c + 1, 1 - slot)
                    if e == 1 and exists(c + 2 - 2 * more):
                        norm(c + 2, slot)
                    if e == 3 and exists(c + 2 - 2 * more):
                        scale(c + 2)
                    if e == 5 and not is_first(c):
                        residual(c - 1)
                    beside(c, e, 1)
                    if e == 0 and not is_first(c):
                        gates(c, GATE_PLACES[-1], GATE_STEPS)

            if prepare:
                prepare.dve_consts(dve)
            if not made:
                norm(0, 0)
                scale(0)
            if prepare:
                prepare.low(dve, nc.vector, "router")
                prepare.low(dve, nc.vector, "w1")
            if not made:
                split_x(0, 0)
            if prepare:
                prepare.low(dve, nc.vector, "w3")
                dve.wait_ge(prepare.bias_loaded, DMA)
                prepare.wait_pool_tables(dve)
            if not made:
                norm(1, 1)
                scale(1)
            gates(0, 0, GATE_STEPS)
            if prepare:
                prepare.low(dve, nc.vector, "attn", y_bank)
            run_pairs(dve, chunk)
            if prepare:
                select_heads(nc, consts, prepare.dve_tables)
            residual(CHUNKS - 1)

        @block.tensor
        def _(pe):
            def turn_x(c):
                pe.wait_ge(ln_done, norm0 + c + 1)
                wait_count(pe, x_added, c - 2)
                for t in range(TILES):
                    last = nc.tensor.transpose(t_bank[:, t * P:(t + 1) * P], xn[:, t, :], ident[:, :])
                last.then_inc(xt_done, 1)

            def router(c, slot):
                wait_count(pe, xhi_done, c + 1 - made)
                wait_count(pe, xlo_done, c + 1 - made)
                wait_count(pe, gate_t_done, c)
                for t in range(TILES):
                    tile = slice(t * P, (t + 1) * P)
                    pairs = ((xt_hi, w["router_hi"]), (xt_hi, w["router_lo"]), (xt_lo, w["router_hi"]))
                    for i, (xs, ws) in enumerate(pairs):
                        last = nc.tensor.matmul(logits[:, t, :], xs[slot][:, tile], ws[:, :],
                                                start=(i == 0), stop=(i == 2))
                last.then_inc(logits_done, 1)

            def turn_gates(c):
                pe.wait_ge(gate_step, (c + 1) * GATE_STEPS)
                for t in range(TILES):
                    last = nc.tensor.transpose(gate_tp[:, t * P:(t + 1) * P], gate_parts[:, t, :],
                                               consts["ident16"][:, :])
                last.then_inc(gate_tp_done, 1)

            def up(c, slot, e):
                n, k = c * STEPS + e, (slot + e) % 2
                if e == 0:
                    wait_count(pe, xhi_done, c + 1 - made)
                    wait_count(pe, xlo_done, c + 1 - made)
                for dst, name, free, done in ((a_bank, "w1", silu_done, a_done), (b_bank, "w3", prod_done, b_done)):
                    if prepare and is_first(c) and e == 0:
                        prepare.wait_split(pe, name)
                    wait_count(pe, free, n - 1)
                    pairs = ((w[name + "_hi"], xt_hi), (w[name + "_lo"], xt_hi), (w[name + "_hi"], xt_lo))
                    for i, (ws, xs) in enumerate(pairs):
                        last = nc.tensor.matmul(dst[k][:, :], ws[:, e, :], xs[slot][:, :], start=(i == 0), stop=(i == 2))
                    last.then_inc(done, 1)
                    if name == "w1" and e > 1:
                        spread_gate(c, slot, e - 1)
                    elif name == "w1" and e == 0 and not is_first(c):
                        spread_gate(c - 1, 1 - slot, STEPS - 1)

            def spread_gate(c, slot, e):
                if e == 1:
                    pe.wait_ge(gate_t_done, c + 1)
                wait_count(pe, h_done, c * EXPERTS + e - 1)
                nc.tensor.matmul(gate_bank[:, :], select_gate[:, e - 1, :], gate_t[slot][:, :],
                                 start=True, stop=True).then_inc(gate_b_done, 1)

            def down(c, slot, e):
                n, k = c * STEPS + e, e % 3
                pe.wait_ge(hhi_done, n + 1)
                pe.wait_ge(hlo_done, n + 1)
                if prepare and is_first(c) and e == 0:
                    prepare.wait_split(pe, "attn")
                    prepare.wait_split(pe, "w2")
                if e == 0:
                    wait_count(pe, yt_done, c)
                pairs = ((w["w2_hi"], h_hi), (w["w2_lo"], h_hi), (w["w2_hi"], h_lo))
                for i, (ws, hs) in enumerate(pairs):
                    last = nc.tensor.matmul(y_bank[:, :], ws[:, e, :], hs[k][:, :],
                                            start=(e == 0 and i == 0), stop=(e == STEPS - 1 and i == 2))
                last.then_inc(w2_done, 1)

            def turn_y(c):
                pe.wait_ge(yt_done, c + 1)
                pe.wait_ge(xlo_done, min(c + 2, CHUNKS + more) - made if isinstance(c, int) else c + 2 - made)
                for t in range(TILES):
                    last = nc.tensor.transpose(t_bank[:, t * P:(t + 1) * P], yt[:, t * P:(t + 1) * P], ident[:, :])
                last.then_inc(y_tok_done, 1)

            def chunk(c, slot):
                for e in range(STEPS):
                    up(c, slot, e)
                    if e == 0 and exists(c + 1 - more):
                        turn_x(c + 1)
                    if e >= LAG:
                        down(c, slot, e - LAG)
                    elif not is_first(c):
                        down(c - 1, 1 - slot, STEPS - LAG + e)
                    if e == 1:
                        turn_gates(c)
                    if e == 2 and not is_last(c):
                        router(c + 1, 1 - slot)
                    if e == 4 and not is_first(c):
                        turn_y(c - 1)

            if prepare:
                pe.wait_ge(prepare.ident_done, 1)
            if not made:
                turn_x(0)
            if prepare:
                prepare.wait_split(pe, "router")
            router(0, 0)
            if prepare:
                prepare.turn_attn(pe, y_bank)
                prepare.wait_dve_tables(pe)
            run_pairs(pe, chunk)
            spread_gate(CHUNKS - 1, 1, STEPS - 1)
            for e in range(STEPS - LAG, STEPS):
                down(CHUNKS - 1, 1, e)
            turn_y(CHUNKS - 1)

        @block.scalar
        def _(act):
            def split_x(c, slot):
                act.wait_ge(xt_done, c + 1 - made)
                wait_count(act, b_done, (c - 1) * STEPS)
                nc.scalar.activation(xt_hi[slot][:, :], t_bank[:, :], ACT.Copy).then_inc(xhi_done, 1)

            def expd(c):
                act.wait_ge(gate_step, c * GATE_STEPS + 2)
                nc.scalar.activation(g["expd"][:, :, :], g["shifted"][:, :, :], ACT.Exp).then_inc(expd_done, 1)

            def take_gates(c, slot):
                act.wait_ge(gate_tp_done, c + 1)
                wait_count(act, gate_b_done, (c - 1) * EXPERTS)
                nc.scalar.activation(gate_t[slot][:, :], gate_tp, ACT.Copy).then_inc(gate_t_done, 1)

            def silu_a(c, slot, e):
                n, k = c * STEPS + e, (slot + e) % 2
                act.wait_ge(a_done, n + 1)
                wait_count(act, prod_done, n - 1)
                nc.scalar.activation(silu[k][:, :], a_bank[k][:, :], ACT.Silu).then_inc(silu_done, 1)

            def split_h(c, slot, e):
                n, k = c * STEPS + e, e % 3
                if e == 0:
                    act.wait_ge(prod_done, n + 1)
                else:
                    act.wait_ge(h_done, c * EXPERTS + e)
                wait_count(act, w2_done, n - 2)
                wait_count(act, hlo_done, n - 2)
                nc.scalar.activation(h_hi[k][:, :], h[k][:, :], ACT.Copy).then_inc(hhi_done, 1)

            def take_y(c):
                act.wait_ge(w2_done, (c + 1) * STEPS)
                wait_count(act, y_tok_done, c)
                nc.scalar.activation(yt[:, :], y_bank[:, :], ACT.Copy, scale=0.5).then_inc(yt_done, 1)

            def chunk(c, slot):
                for e in range(STEPS):
                    if e == 3 and not is_first(c):
                        take_y(c - 1)
                    silu_a(c, slot, e)
                    if e == 0 and exists(c + 1 - more):
                        split_x(c + 1, 1 - slot)
                    if e == 1:
                        take_gates(c, slot)
                    if e > 0:
                        split_h(c, slot, e - 1)
                    elif not is_first(c):
                        split_h(c - 1, 1 - slot, STEPS - 1)
                    if e == 3 and not is_last(c):
                        expd(c + 1)

            if prepare:
                prepare.high(act, "router")
                prepare.high(act, "w1")
            if not made:
                split_x(0, 0)
            if prepare:
                prepare.high(act, "w3")
                prepare.high(act, "w2")
            expd(0)
            if prepare:
                prepare.high(act, "attn", y_bank)
            run_pairs(act, chunk)
            split_h(CHUNKS - 1, 1, STEPS - 1)
            take_y(CHUNKS - 1)

        @block.gpsimd
        def _(pool):
            def low_part(c, e):
                n, k = c * STEPS + e, e % 3
                pool.wait_ge(hhi_done, n + 1)
                wait_count(pool, w2_done, n - 2)
                nc.gpsimd.tensor_tensor(h_lo[k][:, :], h[k][:, :], h_hi[k][:, :], ALU.subtract).then_inc(hlo_done, 1)

            def chunk(c, slot):
                for e in range(STEPS):
                    low_part(c, e)
                    if e == 1 and exists(c + 2 - 2 * more):
                        norm_root(pool, nc, norm0 + c + 2, buf, ln_step, ln_rooted)

            if prepare:
                prepare.pool_consts(pool)
                prepare.wait_pool_tables(pool)
            if not made:
                norm_root(pool, nc, 0, buf, ln_step, ln_rooted)
            if prepare:
                prepare.low(pool, nc.gpsimd, "w2")
            if not made:
                norm_root(pool, nc, 1, buf, ln_step, ln_rooted)
            run_pairs(pool, chunk)


def select_heads(nc, consts, done):
    ident = consts["ident"][:, :].rearrange("p (g j d) -> p g j d", g=GROUPS, j=UNITS)
    half = GROUPS // 2
    for name, low_place in (("sel_q", 2), ("sel_k", 1)):
        table = consts[name][:, :, :].rearrange("p g (j r) -> p g j r", r=ROWS)
        for place in range(ROWS // HEAD):
            for first in (0, half):
                dst = table[:, first:first + half, :, place * HEAD:(place + 1) * HEAD]
                if place == MAX_ROW // HEAD:
                    nc.vector.tensor_scalar(dst, ident[:, first:first + half, :, :], 0.0, None,
                                            ALU.mult).then_inc(done, 1)
                else:
                    src = half - first if place == low_place else first
                    nc.vector.tensor_copy(dst, ident[:, src:src + half, :, :]).then_inc(done, 1)
    nc.vector.tensor_reduce(consts["max_row"][:, :], consts["ident"][:, MAX_ROW:P:ROWS], AX.X,
                            ALU.add).then_inc(done, 1)


PLACES = (((), ("q",), ("k",)), (("o10",), ("o11",), ("Q00",)), (("K00",), ("Q01",), ("K01",)),
          (("m10", "m11"), ("y1",), ()),
          (("z1",), ("Q10",), ("K10",)), (("o00",), ("o01",), ("Q11",)), (("K11",), ("y0",), ("v",)),
          (("m00", "m01"), ("x",), ("z0",)))
JOBS = [name for unit in PLACES for place in unit for name in place]
SHIFT = {n: -2 if n == "x" else -1 if n in ("m00", "m01") or n[0] in "qkQKv" else 1 if n in ("o10", "o11", "y1", "z1")
         else 0 for n in JOBS}


def has_job(name, c):
    return exists(c - 1) if name == "x" else exists(c)


def jobs_of(turn):
    return [n for n in JOBS if has_job(n, turn - SHIFT[n])]


def job_at(c, name):
    if isinstance(c, int):
        turn = c + SHIFT[name]
        n = sum(len(jobs_of(t)) for t in range(-2, turn)) + jobs_of(turn).index(name)
        return n % 2, n // 2
    n = sum(len(jobs_of(t)) for t in range(-2, 1)) + (SHIFT[name] - 1) * len(JOBS) + JOBS.index(name)
    return n % 2, c * (len(JOBS) // 2) + n // 2


def attention_phase(nc, x, consts, w, norms):
    with ExitStack() as ctx:
        def sb(name, shape, dt):
            return ctx.enter_context(nc.sbuf_tensor(f"{name}_at", shape, dt))

        def bank(name):
            return ctx.enter_context(nc.psum_tensor(f"{name}_at", [P, CHUNK], F32))

        def sem(name):
            return ctx.enter_context(nc.semaphore(f"{name}_at"))

        ident, ident16 = consts["ident"], consts["ident16"]
        buf, xn = norms, norms["xn"]
        ln_step, ln_rooted, ln_done = norms["step"], norms["rooted"], norms["done"]
        norm0 = CHUNKS
        xt_hi, xt_lo = norms["xt_hi"][0], norms["xt_lo"][0]
        stack = {m: [sb(f"{m}_stack{half}", [P, CHUNK], F16) for half in range(2)] for m in "qk"}
        half_rows = (slice(0, P // 2), slice(P // 2, P))
        q_pack = [sb(f"q_pack{s}", [P, GROUPS, CHUNK], F16) for s in range(2)]
        k_pack = [sb(f"k_pack{s}", [P, GROUPS, CHUNK], F16) for s in range(2)]
        v_ones = [sb(f"v_ones{s}", [P, TILES, HEADS, ROWS], F32) for s in range(2)]
        neg_max = [sb(f"neg_max{b}", [P, 2, GROUPS, UNITS, ROWS], F16) for b in range(2)]
        probs = [sb(f"probs{s}", [P, 3, CHUNK], F32) for s in range(2)]
        o_t = [sb(f"o_t{s}", [P, UNITS, SEQ], F32) for s in range(2)]
        inv = sb("inv", [P, 2, UNITS, GROUPS], F32)
        y = sb("y", [P, 2, P], F32)
        yt_hi, yt_lo = sb("yt_hi", [P, SEQ], F16), sb("yt_lo", [P, SEQ], F16)

        score_bank = [bank(f"score{s}") for s in range(2)]
        prob_bank = [bank(f"prob{i}") for i in range(3)]
        o_bank = bank("o")
        job_bank = [bank(f"job{s}") for s in range(2)]

        job_written = [sem(f"job_written{s}") for s in range(2)]
        job_taken = [sem(f"job_taken{s}") for s in range(2)]
        buffers_set = sem("buffers_set")
        xhi_done, qkhi_done, yhi_done, inv_done = (sem(n) for n in ("xhi_done", "qkhi_done", "yhi_done", "inv_done"))
        mask_begun = sem("mask_begun")
        scored, max_done = sem("scored"), sem("max_done")
        st_done, exp_done, masked, pv_done, o_done = (
            sem(n) for n in ("st_done", "exp_done", "masked", "pv_done", "o_done"))

        block = ctx.enter_context(nc.Block())

        def take(eng, c, name):
            k, before = job_at(c, name)
            eng.wait_ge(job_written[k], before + 1)
            return job_bank[k], job_taken[k]

        def wait_taken(eng, c, name):
            k, before = job_at(c, name)
            eng.wait_ge(job_taken[k], before + 1)

        def unit_ahead(c, slot, b, j):
            at = b * UNITS + j + UNITS + 1
            later, at = divmod(at, 2 * UNITS)
            return (c + later, (slot + later) % 2, *divmod(at, UNITS)) if exists(c + later) else None

        def packed(pack, name):
            b, half = int(name[1]), int(name[2])
            return pack[:, 2 * half:2 * half + 2, b * SEQ:(b + 1) * SEQ]

        def unit_rows(j):
            return slice(ROWS * j, ROWS * (j + 1))

        def turn_jobs(do, c, slot, names):
            for name in names:
                if has_job(name, c - SHIFT[name]):
                    do(c - SHIFT[name], (slot - SHIFT[name]) % 2, name)

        @block.tensor
        def _(pe):
            def begin(c, name):
                k, before = job_at(c, name)
                wait_count(pe, job_taken[k], before)
                return job_bank[k], job_written[k]

            def product(dst, pairs):
                for n, (stationary, moving) in enumerate(pairs):
                    last = nc.tensor.matmul(dst, stationary, moving, start=(n == 0), stop=(n == 2))
                return last

            w_hi, w_lo = w["attn_hi"], w["attn_lo"]

            def job(c, slot, name):
                kind = name[0]
                if kind == "x":
                    pe.wait_ge(ln_done, norm0 + c + 1)
                    dst, done = begin(c, name)
                    for t in range(TILES):
                        last = nc.tensor.transpose(dst[:, t * P:(t + 1) * P], xn[:, t, :], ident[:, :])
                elif kind in "qk":
                    if not is_first(c):
                        wait_taken(pe, c, "x")
                    dst, done = begin(c, name)
                    i = "qk".index(kind)
                    last = product(dst[:, :], ((w_hi[:, i, :], xt_hi[:, :]), (w_lo[:, i, :], xt_hi[:, :]),
                                               (w_hi[:, i, :], xt_lo[:, :])))
                elif kind in "QK":
                    m, b, half = kind.lower(), int(name[1]), int(name[2])
                    wait_taken(pe, c, m)
                    dst, done = begin(c, name)
                    tokens = slice(b * SEQ, (b + 1) * SEQ)
                    for i in range(2):
                        tile = dst[:, i * SEQ:(i + 1) * SEQ]
                        last = nc.tensor.matmul(tile, consts["sel_" + m][:, 2 * half + i, :],
                                                stack[m][half][:, tokens], start=True, stop=True)
                elif kind == "v":
                    dst, done = begin(c, name)
                    for t in range(TILES):
                        tile = slice(t * P, (t + 1) * P)
                        last = product(dst[:, tile], ((xt_hi[:, tile], w_hi[:, 2, :]), (xt_hi[:, tile], w_lo[:, 2, :]),
                                                      (xt_lo[:, tile], w_hi[:, 2, :])))
                elif kind == "o":
                    b, t = int(name[1]), int(name[2])
                    pe.wait_ge(o_done, c * 2 * UNITS + (b + 1) * UNITS)
                    dst, done = begin(c, name)
                    for j in range(UNITS):
                        last = nc.tensor.transpose(dst[:, j * P:(j + 1) * P], o_t[b][:, j, t * P:(t + 1) * P],
                                                   ident[:, :])
                elif kind == "y":
                    b = int(name[1])
                    wait_taken(pe, c, f"o{b}0")
                    wait_taken(pe, c, f"o{b}1")
                    dst, done = begin(c, name)
                    for t in range(2):
                        last = nc.tensor.transpose(dst[:, t * P:(t + 1) * P], y[:, t, :], ident[:, :])
                elif kind == "z":
                    wait_taken(pe, c, "y" + name[1])
                    dst, done = begin(c, name)
                    for t in range(2):
                        tile = slice(t * P, (t + 1) * P)
                        last = product(dst[:, tile], ((yt_hi[:, tile], w_hi[:, 3, :]), (yt_hi[:, tile], w_lo[:, 3, :]),
                                                      (yt_lo[:, tile], w_hi[:, 3, :])))
                elif kind == "m":
                    b, t = int(name[1]), int(name[2])
                    pe.wait_ge(max_done, c * 24 + (b + 1) * 12)
                    dst, done = begin(c, name)
                    for g in range(GROUPS):
                        last = nc.tensor.matmul(dst[:, g * P:(g + 1) * P],
                                                neg_max[b][:, t, g, :, :].rearrange("p j r -> p (j r)"), ident16[:, :],
                                                start=True, stop=True)
                last.then_inc(done, 1)

            def scores(c, slot, b, j, parts=(0, 1, 2)):
                if j == 0 and parts[0] == 0:
                    wait_taken(pe, c, f"Q{b}1")
                    wait_taken(pe, c, f"K{b}1")
                rows, first = unit_rows(j), b * SEQ
                for i in parts:
                    n = c * 24 + b * 12 + 3 * j + i
                    wait_count(pe, max_done, n - 1)
                    dst = score_bank[(3 * j + i) % 2]
                    groups = range(GROUPS) if i == 0 else range(2 * i - 2, 2 * i)
                    keys = P if i == 0 else SEQ
                    view = dst[:, :].rearrange("p (h k) -> p h k", k=keys)
                    nc.tensor.matmul(view[:, :, keys - P:keys], consts["ident_b"][:, :],
                                     consts["causal"][:, :].unsqueeze(1).to_broadcast([P, len(groups), P]),
                                     start=True, stop=False, skip_group_check=True)
                    q0 = first + (0 if i == 0 else P)
                    for h, g in enumerate(groups):
                        last = nc.tensor.matmul(view[:, h, :], q_pack[slot][rows, g, q0:q0 + P],
                                                k_pack[slot][rows, g, first:first + keys], start=False,
                                                stop=(h == len(groups) - 1), skip_group_check=True)
                    last.then_inc(scored, 1)

            def scores_t(c, slot, b, j):
                rows, first = unit_rows(j), b * SEQ
                unit = c * 2 * UNITS + b * UNITS + j
                if j == 0:
                    wait_taken(pe, c, f"m{b}0")
                    wait_taken(pe, c, f"m{b}1")
                for i in range(3):
                    wait_count(pe, exp_done, unit * 3 - 2 + i)
                    pe.wait_ge(buffers_set, 1)
                    keys = slice(first, first + P) if i < 2 else slice(first + P, first + SEQ)
                    queries = slice(keys.start, first + SEQ)
                    width = queries.stop - queries.start
                    for h, g in enumerate(range(2 * i, 2 * i + 2) if i < 2 else range(GROUPS)):
                        last = nc.tensor.matmul(prob_bank[i][:, h * width:(h + 1) * width],
                                                k_pack[slot][rows, g, keys], q_pack[slot][rows, g, queries],
                                                start=True, stop=True)
                    last.then_inc(st_done, 1)

            def weigh(c, slot, b, j):
                unit = c * 2 * UNITS + b * UNITS + j
                if j == 0 and b == 0:
                    wait_taken(pe, c, "v")
                pe.wait_ge(masked, unit * 2 + 2)
                wait_count(pe, o_done, unit)
                for t in range(2):
                    for g in range(GROUPS):
                        src = (probs[j % 2][:, g // 2, (g % 2) * SEQ:(g % 2 + 1) * SEQ] if t == 0
                               else probs[j % 2][:, 2, g * P:(g + 1) * P])
                        last = nc.tensor.matmul(o_bank[g * ROWS:(g + 1) * ROWS, t * P:SEQ],
                                                v_ones[slot][:, 2 * b + t, GROUPS * g + j, :], src,
                                                start=(t == 0), stop=(t == 1), skip_group_check=True)
                last.then_inc(pv_done, 1)

            def turn(c, slot):
                for b in range(2):
                    for j in range(UNITS):
                        scores_t(c, slot, b, j)
                        places = PLACES[b * UNITS + j]
                        turn_jobs(job, c, slot, places[0])
                        ahead = unit_ahead(c, slot, b, j)
                        if ahead:
                            scores(*ahead, parts=(0, 1))
                        turn_jobs(job, c, slot, places[1])
                        if j > 0:
                            weigh(c, slot, b, j - 1)
                        elif b == 1:
                            weigh(c, slot, 0, UNITS - 1)
                        elif exists(c - 1):
                            weigh(c - 1, 1 - slot, 1, UNITS - 1)
                        if ahead:
                            scores(*ahead, parts=(2,))
                        turn_jobs(job, c, slot, places[2])

            turn_jobs(job, -1, 1, JOBS[:-4])
            for j in range(UNITS):
                scores(0, 0, 0, j)
            turn_jobs(job, -1, 1, JOBS[-4:])
            scores(0, 0, 1, 0)
            run_pairs(pe, turn)
            weigh(CHUNKS - 1, 1, 1, UNITS - 1)
            turn_jobs(job, CHUNKS, 0, JOBS)

        @block.vector
        def _(dve):
            def norm(c):
                if isinstance(c, int) and c >= CHUNKS:
                    wait_taken(dve, c - CHUNKS, "z1")
                norm_stats(dve, nc, norm0 + c, chunk_rows(x, c), buf, ln_step, ln_done)

            def scale(c):
                wait_taken(dve, c - 1, "x")
                norm_scale(dve, nc, norm0 + c, chunk_rows(x, c), buf, ln_rooted, ln_done)

            def job(c, slot, name):
                kind = name[0]
                if kind in "Kv" or (kind == "Q" and name[2] == "1"):
                    return
                src, done = take(dve, c, name)
                if kind == "x":
                    dve.wait_ge(xhi_done, c)
                    last = nc.vector.tensor_tensor(xt_lo[:, :], src[:, :], xt_hi[:, :], ALU.subtract)
                elif kind in "qk":
                    for half, rows in enumerate(half_rows):
                        dve.wait_ge(qkhi_done, c * 4 + (1 if kind == "q" else 3) + half)
                        last = nc.vector.tensor_tensor(stack[kind][half][half_rows[1 - half], :], src[rows, :],
                                                       stack[kind][half][rows, :], ALU.subtract)
                elif kind == "Q":
                    wait_count(dve, st_done, (c - 1) * 6 * UNITS)
                    last = nc.vector.tensor_copy(packed(q_pack[slot], name),
                                                 src[:, :].rearrange("p (g n) -> p g n", n=SEQ))
                elif kind == "m":
                    first = int(name[1]) * SEQ + int(name[2]) * P
                    q = q_pack[slot][:, :, first:first + P]
                    last = nc.vector.tensor_tensor(q, src[:, :].rearrange("p (g q) -> p g q", q=P), q, ALU.add)
                elif kind == "o":
                    b, t = int(name[1]), int(name[2])
                    o = src[:, :].rearrange("p (j g r) -> p j g r", j=UNITS, r=ROWS)
                    nc.vector.reciprocal(inv[:, t, :, :], o[:, :, :, HEAD]).then_inc(inv_done, 1)
                    dve.wait_ge(inv_done, c * 4 + 2 * b + t + 1)
                    last = nc.vector.tensor_tensor(y[:, t, :].rearrange("p (g j d) -> p j g d", j=UNITS, d=HEAD),
                                                   o[:, :, :, 0:HEAD],
                                                   inv[:, t, :, :].unsqueeze(3).to_broadcast([P, UNITS, GROUPS, HEAD]),
                                                   ALU.mult)
                elif kind == "y":
                    dve.wait_ge(yhi_done, c * 2 + int(name[1]) + 1)
                    last = nc.vector.tensor_tensor(yt_lo[:, :], src[:, 0:SEQ], yt_hi[:, :], ALU.subtract)
                elif kind == "z":
                    rows = x[:, bass.ds(c * TILES + 2 * int(name[1]), 2), :]
                    last = nc.vector.tensor_tensor(rows, rows, src[:, 0:SEQ].rearrange("p (t d) -> p t d", d=P),
                                                   ALU.add)
                last.then_inc(done, 1)

            def maxima(c, b, j, parts=(0, 1, 2)):
                for i in parts:
                    n = c * 24 + b * 12 + 3 * j + i
                    dve.wait_ge(scored, n + 1)
                    src = score_bank[(3 * j + i) % 2][:, :].rearrange("p (h k) -> p h k", k=P if i == 0 else SEQ)
                    dst = (neg_max[b][:, 0, :, j, MAX_ROW] if i == 0 else neg_max[b][:, 1, 2 * i - 2:2 * i, j, MAX_ROW])
                    nc.vector.tensor_reduce(dst, src, AX.X, ALU.max, negate=True).then_inc(max_done, 1)

            def turn(c, slot):
                for b in range(2):
                    for j in range(UNITS):
                        places = PLACES[b * UNITS + j]
                        turn_jobs(job, c, slot, places[0])
                        ahead = unit_ahead(c, slot, b, j)
                        if ahead:
                            maxima(ahead[0], *ahead[2:], parts=(0, 1))
                        turn_jobs(job, c, slot, places[1])
                        if ahead:
                            maxima(ahead[0], *ahead[2:], parts=(2,))
                        if b == 1 and j == 1:
                            norm(c + 2)
                        if b == 1 and j == 2:
                            scale(c + 2)
                        turn_jobs(job, c, slot, places[2])

            for s in range(2):
                nc.vector.memset(neg_max[s][:, :, :, :, :].rearrange("p a b c d -> p (a b c d)"), 0.0)
                v = v_ones[s][:, :, :, :].rearrange("p t h r -> p (t h) r")
                nc.vector.memset(v[:, :, HEAD + 1:ROWS], 0.0)
                last = nc.vector.memset(v[:, :, HEAD:HEAD + 1], 1.0)
            last.then_inc(buffers_set, 1)
            turn_jobs(job, -1, 1, JOBS[:-4])
            dve.wait_ge(buffers_set, 1)
            for j in range(UNITS):
                maxima(0, 0, j)
            turn_jobs(job, -1, 1, JOBS[-4:])
            maxima(0, 1, 0)
            run_pairs(dve, turn)
            turn_jobs(job, CHUNKS, 0, JOBS)

        @block.scalar
        def _(act):
            def job(c, slot, name):
                kind = name[0]
                if kind in "moz" or (kind == "Q" and name[2] == "0"):
                    return
                if kind == "y":
                    b = int(name[1])
                    if b == 1:
                        wait_taken(act, c, "z0")
                    elif not is_first(c):
                        wait_taken(act, c - 1, "z1")
                src, done = take(act, c, name)
                if kind == "x":
                    nc.scalar.activation(xt_hi[:, :], src[:, :], ACT.Copy).then_inc(xhi_done, 1)
                elif kind in "qk":
                    for half, rows in enumerate(half_rows):
                        nc.scalar.activation(stack[kind][half][rows, :], src[rows, :], ACT.Copy).then_inc(qkhi_done, 1)
                elif kind == "Q":
                    wait_count(act, st_done, (c - 1) * 6 * UNITS)
                    nc.scalar.activation(packed(q_pack[slot], name), src[:, :].rearrange("p (g n) -> p g n", n=SEQ),
                                         ACT.Copy).then_inc(done, 1)
                elif kind == "K":
                    nc.scalar.activation(packed(k_pack[slot], name), src[:, :].rearrange("p (g n) -> p g n", n=SEQ),
                                         ACT.Identity, bias=consts["max_row"][:, :]).then_inc(done, 1)
                elif kind == "v":
                    nc.scalar.activation(v_ones[slot][:, :, :, 0:HEAD],
                                         src[:, :].rearrange("p (t h d) -> p t h d", t=TILES, d=HEAD),
                                         ACT.Copy).then_inc(done, 1)
                elif kind == "y":
                    nc.scalar.activation(yt_hi[:, :], src[:, 0:SEQ], ACT.Copy).then_inc(yhi_done, 1)

            def exponents(c, b, j):
                unit = c * 2 * UNITS + b * UNITS + j
                for i in range(3):
                    act.wait_ge(st_done, unit * 3 + i + 1)
                    if i == 0:
                        wait_count(act, pv_done, unit - 1)
                    nc.scalar.activation(probs[j % 2][:, i, :], prob_bank[i][:, :], ACT.Exp,
                                         scale=SCALE).then_inc(exp_done, 1)

            def take_o(c, b, j):
                unit = c * 2 * UNITS + b * UNITS + j
                act.wait_ge(pv_done, unit + 1)
                nc.scalar.activation(o_t[b][:, j, :], o_bank[:, 0:SEQ], ACT.Copy).then_inc(o_done, 1)

            def turn(c, slot):
                for b in range(2):
                    for j in range(UNITS):
                        exponents(c, b, j)
                        places = PLACES[b * UNITS + j]
                        turn_jobs(job, c, slot, places[0])
                        turn_jobs(job, c, slot, places[1])
                        if j > 0:
                            take_o(c, b, j - 1)
                        elif b == 1:
                            take_o(c, 0, UNITS - 1)
                        elif exists(c - 1):
                            take_o(c - 1, 1, UNITS - 1)
                        turn_jobs(job, c, slot, places[2])

            act.wait_ge(buffers_set, 1)
            turn_jobs(job, -1, 1, JOBS)
            run_pairs(act, turn)
            take_o(CHUNKS - 1, 1, UNITS - 1)
            turn_jobs(job, CHUNKS, 0, JOBS)

        @block.gpsimd
        def _(pool):
            def mask(c, b, j):
                unit = c * 2 * UNITS + b * UNITS + j
                for i in range(2):
                    pool.wait_ge(exp_done, unit * 3 + 2 + i)
                    pool.sem_inc(mask_begun, 1)
                    p = (probs[j % 2][:, 0:2, :].rearrange("p i (h q) -> p (i h) q", q=SEQ)[:, :, 0:P] if i == 0
                         else probs[j % 2][:, 2, :].rearrange("p (h q) -> p h q", q=P))
                    nc.gpsimd.affine_select(out=p, in_=p, compare_op=ALU.is_ge, fill=0.0, base=0,
                                            pattern=[[0, GROUPS], [1, P]], channel_multiplier=-1).then_inc(masked, 1)

            def turn(c, slot):
                for b in range(2):
                    for j in range(UNITS):
                        mask(c, b, j)
                        if b == 1 and j == 1:
                            norm_root(pool, nc, norm0 + c + 2, buf, ln_step, ln_rooted)

            run_pairs(pool, turn)



def macaron_kernel(nc, L0_attn_x, L0_attn_W_Q, L0_attn_W_K, L0_attn_W_V, L0_attn_W_O, L0_ffn_router_w,
                   L0_ffn_expert_bias, L0_ffn_w1, L0_ffn_w2, L0_ffn_w3, L0_ffn_sw1, L0_ffn_sw2, L0_ffn_sw3, out):
    with ExitStack() as ctx:
        def sb(name, shape, dt):
            return ctx.enter_context(nc.sbuf_tensor(name, shape, dt))

        x = sb("x", [P, CHUNKS * TILES, P], F32)
        consts = {
            "ident": sb("ident", [P, P], F32), "ident16": sb("ident16", [P, P], F16),
            "ident_b": sb("ident_b", [P, P], BF16), "causal": sb("causal", [P, P], BF16),
            "bias": sb("bias", [P, EXPERTS], F32), "order": sb("order", [P, EXPERTS], F32),
            "power": sb("power", [P, TILES], F32), "eps": sb("eps", [P, TILES], F32),
            "max_row": sb("max_row", [P, 1], F32),
            "select_gate": sb("select_gate", [2 * EXPERTS, EXPERTS, P], F16),
        }
        for n in ("sel_q", "sel_k"):
            consts[n] = sb(n, [P, GROUPS, P], F16)
        w = {f"{n}_{part}": sb(f"{n}_{part}", [P, STEPS, P], F16)
             for n in ("w1", "w3", "w2") for part in ("hi", "lo")}
        for part in ("hi", "lo"):
            w["router_" + part] = sb("router_" + part, [P, EXPERTS], F16)
            w["attn_" + part] = sb("attn_" + part, [P, 4, P], F16)
        ffn = {"w1": (L0_ffn_sw1, L0_ffn_w1), "w3": (L0_ffn_sw3, L0_ffn_w3), "w2": (L0_ffn_sw2, L0_ffn_w2)}
        attn = {"wq": L0_attn_W_Q, "wk": L0_attn_W_K, "wv": L0_attn_W_V, "wo": L0_attn_W_O}
        x_dram = L0_attn_x.rearrange("b s d -> (b s) d")
        out_dram = out.rearrange("b s d -> (b s) d")

        norms = {
            "stats": sb("stats", [P, TILES, 6], F32), "moments": sb("moments", [P, TILES, 2], F32),
            "rstd": sb("rstd", [P, TILES], F32), "var_eps": sb("var_eps", [P, TILES], F32),
            "power": consts["power"], "eps": consts["eps"], "spare": sb("spare", [P, 1], F32),
            "xn": sb("xn", [P, TILES, P], F32),
            "xt_hi": [sb(f"xt_hi{s}", [P, CHUNK], F16) for s in range(2)],
            "xt_lo": [sb(f"xt_lo{s}", [P, CHUNK], F16) for s in range(2)],
        }
        for n in ("step", "rooted", "done"):
            norms[n] = ctx.enter_context(nc.semaphore(f"ln_{n}"))

        with ExitStack() as first:
            prepare = WeightPreparation(nc, first, consts, w, ffn, attn, L0_ffn_expert_bias, L0_ffn_router_w)
            ffn_phase(nc, x, consts, w, norms, 0, x_dram, None, prepare)
        attention_phase(nc, x, consts, w, norms)
        ffn_phase(nc, x, consts, w, norms, 1, None, out_dram)


_INS = ['L0_attn_x', 'L0_attn_W_Q', 'L0_attn_W_K', 'L0_attn_W_V', 'L0_attn_W_O', 'L0_ffn_router_w',
        'L0_ffn_expert_bias', 'L0_ffn_w1', 'L0_ffn_w2', 'L0_ffn_w3', 'L0_ffn_sw1', 'L0_ffn_sw2', 'L0_ffn_sw3']
_OUTS = [((32, 256, 128), 'float32')]


def kernel(**inputs):
    import numpy as _np
    import concourse.bacc as _bacc
    from concourse import mybir as _mybir
    from concourse.bass_utils import run_bass_kernel_spmd as _run

    nc = _bacc.Bacc("TRN2", target_bir_lowering=False, num_devices=1)
    arrays, args = {}, []
    for name in _INS:
        a = _np.ascontiguousarray(inputs[name])
        arrays[f"in_{name}_dram"] = a
        args.append(nc.dram_tensor(f"in_{name}_dram", a.shape, _mybir.dt.from_np(a.dtype), kind="ExternalInput").ap())
    for i, (shape, dtype) in enumerate(_OUTS):
        dt = _mybir.dt.from_np(_np.dtype(dtype))
        args.append(nc.dram_tensor(f"out_{i}_dram", shape, dt, kind="ExternalOutput").ap())
    macaron_kernel(nc, *args)
    r = _run(nc, [arrays], core_ids=[0])
    got = tuple(r.results[0][f"out_{i}_dram"] for i in range(len(_OUTS)))
    return got[0]
```
